# Optimizing a Trainium2 kernel written in Bass

```python
import numpy as np
import jax
import jax.numpy as jnp

def _softmax(x, axis=-1):
    return jax.nn.softmax(x, axis=axis)

def _gelu(x):
    return jax.nn.gelu(x, approximate=True)

def _silu(x):
    return jax.nn.silu(x)

def _sigmoid(x):
    return jax.nn.sigmoid(x)

def _layernorm(x, axis=-1, eps=1e-05):
    m = jnp.mean(x, axis=axis, keepdims=True)
    v = jnp.var(x, axis=axis, keepdims=True)
    return (x - m) / jnp.sqrt(v + eps)

def _scatter_add(tgt, idx, src, axis=0):
    return tgt.at[idx].add(src)

def _segment_sum(src, seg, n):
    return jax.ops.segment_sum(src, seg, n)
kernel_name = 'mk_adj_ffn_d1_adj_r2_843f15'

def setup_inputs(seed: int=0):
    np.random.seed(seed)
    _w = jnp.asarray

    def _rec_inputs():
        import jax
        import jax.numpy as jnp
        _gk = jax.random.key(seed)
        x = -0.0001538 + 1 * jax.random.normal(jax.random.fold_in(_gk, 1), (128, 128, 384), jnp.float32)
        _a = jax.random.bernoulli(jax.random.fold_in(_gk, 2), 0.03125, (128, 128, 128))
        _a = jnp.logical_or(_a, jnp.swapaxes(_a, -1, -2))
        _a = jnp.logical_or(_a, jnp.eye(128, dtype=bool))
        _af = _a.astype(jnp.float32)
        _af = _af * jax.random.uniform(jax.random.fold_in(_gk, 3), (128, 128, 128), jnp.float32, 0.05, 4.42607)
        adj = _af
        return (x, adj)
    x, adj = _rec_inputs()

    def _L0_gnn_setup():
        import jax, jax.numpy as jnp
        import numpy as np
        NUM_HEADS = 12
        HIDDEN = 384
        HEAD = HIDDEN // NUM_HEADS
        B, N = (16, 256)
        key = jax.random.key(seed)
        ks = jax.random.split(key, 9)
        s = 0.02
        return {'x': jax.random.normal(ks[0], (B, N, HIDDEN), jnp.float32), 'spatial_encoding': jax.random.normal(ks[1], (B, N, N), jnp.float32), 'edge_encoding': jax.random.normal(ks[2], (B, N, N), jnp.float32), 'Wq': jax.random.normal(ks[3], (HIDDEN, HIDDEN), jnp.float32) * s, 'Wk': jax.random.normal(ks[4], (HIDDEN, HIDDEN), jnp.float32) * s, 'Wv': jax.random.normal(ks[5], (HIDDEN, HIDDEN), jnp.float32) * s, 'bv': jax.random.normal(ks[6], (HIDDEN,), jnp.float32) * s, 'Wo': jax.random.normal(ks[7], (HIDDEN, HIDDEN), jnp.float32) * s, 'bo': jax.random.normal(ks[8], (HIDDEN,), jnp.float32) * s}
    _L0_gnn_all = _L0_gnn_setup()
    _L0_gnn_in = {k: v for k, v in _L0_gnn_all.items() if k in ('Wq', 'Wk', 'Wv', 'bv', 'Wo', 'bo')}
    del _L0_gnn_all

    def _L0_ffn_setup():
        import jax, jax.numpy as jnp
        import numpy as np
        import math
        B, T, C = (8, 1024, 384)
        E = 3
        HD = C // E
        TOPK = 2
        NGLOB = 4

        def _masked_softmax(att, mask):
            att = jnp.where(mask, -jnp.inf, att)
            return jax.nn.softmax(att, axis=-1)
        key = jax.random.key(seed)
        ks = jax.random.split(key, 16)
        s = 0.02
        return {'x': jax.random.normal(ks[0], (B, T, C), jnp.float32), 'Wqk': jax.random.normal(ks[1], (C, 2 * C), jnp.float32) * s, 'bqk': jnp.zeros((2 * C,), jnp.float32), 'Wv': jax.random.normal(ks[2], (E, C, HD), jnp.float32) * s, 'bv': jnp.zeros((E, HD), jnp.float32), 'conv_w': jax.random.normal(ks[3], (HD, 1, 3), jnp.float32) * s, 'conv_b': jnp.zeros((HD,), jnp.float32), 'glob': jax.random.normal(ks[4], (NGLOB, HD), jnp.float32) * 0.02, 'pos_bias': jnp.zeros((64, 64), jnp.float32), 'Wg1': jax.random.normal(ks[5], (C, 32), jnp.float32) * s, 'bg1': jnp.zeros((32,), jnp.float32), 'Wg2': jax.random.normal(ks[6], (32, E), jnp.float32) * s, 'bg2': jnp.zeros((E,), jnp.float32), 'Wp': jax.random.normal(ks[7], (C, C), jnp.float32) * s, 'bp': jnp.zeros((C,), jnp.float32)}
    _L0_ffn_all = _L0_ffn_setup()
    _L0_ffn_in = {k: v for k, v in _L0_ffn_all.items() if k in ('Wqk', 'bqk', 'Wv', 'bv', 'conv_w', 'conv_b', 'glob', 'pos_bias', 'Wg1', 'bg1', 'Wg2', 'bg2', 'Wp', 'bp')}
    del _L0_ffn_all
    return {'x': x, 'adj': adj, 'L0_gnn_Wq': _L0_gnn_in['Wq'], 'L0_gnn_Wk': _L0_gnn_in['Wk'], 'L0_gnn_Wv': _L0_gnn_in['Wv'], 'L0_gnn_bv': _L0_gnn_in['bv'], 'L0_gnn_Wo': _L0_gnn_in['Wo'], 'L0_gnn_bo': _L0_gnn_in['bo'], 'L0_ffn_Wqk': _L0_ffn_in['Wqk'], 'L0_ffn_bqk': _L0_ffn_in['bqk'], 'L0_ffn_Wv': _L0_ffn_in['Wv'], 'L0_ffn_bv': _L0_ffn_in['bv'], 'L0_ffn_conv_w': _L0_ffn_in['conv_w'], 'L0_ffn_conv_b': _L0_ffn_in['conv_b'], 'L0_ffn_glob': _L0_ffn_in['glob'], 'L0_ffn_pos_bias': _L0_ffn_in['pos_bias'], 'L0_ffn_Wg1': _L0_ffn_in['Wg1'], 'L0_ffn_bg1': _L0_ffn_in['bg1'], 'L0_ffn_Wg2': _L0_ffn_in['Wg2'], 'L0_ffn_bg2': _L0_ffn_in['bg2'], 'L0_ffn_Wp': _L0_ffn_in['Wp'], 'L0_ffn_bp': _L0_ffn_in['bp']}

def reference(x, adj, L0_gnn_Wq, L0_gnn_Wk, L0_gnn_Wv, L0_gnn_bv, L0_gnn_Wo, L0_gnn_bo, L0_ffn_Wqk, L0_ffn_bqk, L0_ffn_Wv, L0_ffn_bv, L0_ffn_conv_w, L0_ffn_conv_b, L0_ffn_glob, L0_ffn_pos_bias, L0_ffn_Wg1, L0_ffn_bg1, L0_ffn_Wg2, L0_ffn_bg2, L0_ffn_Wp, L0_ffn_bp):
    import jax
    import jax.numpy as jnp

    def _L0_gnn_ref(x, spatial_encoding, edge_encoding, Wq, Wk, Wv, bv, Wo, bo):
        import jax, jax.numpy as jnp
        import numpy as np
        NUM_HEADS = 12
        HIDDEN = 384
        HEAD = HIDDEN // NUM_HEADS
        B, N = (16, 256)
        b, n, h = x.shape
        scale = jnp.asarray(HIDDEN, x.dtype) ** (-0.5)
        q = (x @ Wq.T).reshape(b, n, NUM_HEADS, HEAD)
        k = (x @ Wk.T).reshape(b, n, NUM_HEADS, HEAD)
        v = (x @ Wv.T + bv).reshape(b, n, NUM_HEADS, HEAD)
        bias = (spatial_encoding + edge_encoding)[:, None]
        scores = jnp.einsum('bqhd,bkhd->bhqk', q, k) * scale + bias
        row_nonzero = jnp.any(scores != 0, axis=-1, keepdims=True)
        scores = jnp.where(row_nonzero, scores, -jnp.inf)
        p = jax.nn.softmax(scores, axis=-1)
        p = jnp.nan_to_num(p)
        out = jnp.einsum('bhqk,bkhd->bqhd', p, v).reshape(b, n, h)
        return out @ Wo.T + bo

    def _L0_ffn_ref(x, Wqk, bqk, Wv, bv, conv_w, conv_b, glob, pos_bias, Wg1, bg1, Wg2, bg2, Wp, bp):
        import jax, jax.numpy as jnp
        import numpy as np
        import math
        B, T, C = (8, 1024, 384)
        E = 3
        HD = C // E
        TOPK = 2
        NGLOB = 4

        def _masked_softmax(att, mask):
            att = jnp.where(mask, -jnp.inf, att)
            return jax.nn.softmax(att, axis=-1)
        Bx, Tx, Cx = x.shape
        scale = 1.0 / math.sqrt(HD)
        gate = jax.nn.softmax(jax.nn.relu(x @ Wg1 + bg1) @ Wg2 + bg2, axis=-1)
        top_w, top_i = jax.lax.top_k(gate, TOPK)
        top_w = jax.nn.softmax(top_w, axis=-1)
        qk = x @ Wqk + bqk
        q, k = (qk[..., :Cx], qk[..., Cx:])
        q = q.reshape(Bx, Tx, E, HD)
        k = k.reshape(Bx, Tx, E, HD)
        rows = jnp.arange(Tx)[:, None]
        ys = []
        for e in range(E):
            qe = q[:, :, e]
            ke = k[:, :, e]
            ve = x @ Wv[e] + bv[e]
            if e == 0:
                qc = jnp.transpose(qe, (0, 2, 1))
                qc = jax.lax.conv_general_dilated(qc, conv_w, window_strides=(1,), padding=((1, 1),), feature_group_count=HD, dimension_numbers=('NCH', 'OIH', 'NCH'))
                qe = jnp.transpose(qc + conv_b[None, :, None], (0, 2, 1))
            elif e == 1:
                gb = jnp.broadcast_to(glob[None], (Bx, NGLOB, HD))
                ke = jnp.concatenate([ke, gb], axis=1)
                ve = jnp.concatenate([ve, gb], axis=1)
            att = jnp.einsum('btd,bsd->bts', qe, ke) * scale
            if e == 2 and Tx <= 64:
                att = att + pos_bias[:Tx, :Tx][None]
            S = att.shape[-1]
            mask = jnp.arange(S)[None, :] > rows
            att = _masked_softmax(att, mask[None])
            ys.append(jnp.einsum('bts,bsd->btd', att, ve))
        ys = jnp.stack(ys, axis=2)
        w_e = jnp.sum(jax.nn.one_hot(top_i, E, dtype=x.dtype) * top_w[..., None], axis=-2)
        combined = (ys * w_e[..., None]).reshape(Bx, Tx, Cx)
        return combined @ Wp + bp
    x = x + _L0_gnn_ref(_layernorm(x, axis=-1), adj, adj, L0_gnn_Wq, L0_gnn_Wk, L0_gnn_Wv, L0_gnn_bv, L0_gnn_Wo, L0_gnn_bo)
    x = x + _L0_ffn_ref(_layernorm(x, axis=-1), L0_ffn_Wqk, L0_ffn_bqk, L0_ffn_Wv, L0_ffn_bv, L0_ffn_conv_w, L0_ffn_conv_b, L0_ffn_glob, L0_ffn_pos_bias, L0_ffn_Wg1, L0_ffn_bg1, L0_ffn_Wg2, L0_ffn_bg2, L0_ffn_Wp, L0_ffn_bp)
    return x

_drawn_inputs = setup_inputs


def setup_inputs(seed=0):
    import zlib

    import numpy as np

    out = dict(_drawn_inputs(seed))
    spreads = {'L0_ffn_bqk': (0.0, 0.8),
     'L0_ffn_bv': (0.0, 0.502),
     'L0_ffn_conv_b': (0.0, 0.8),
     'L0_ffn_pos_bias': (0.0, 0.1),
     'L0_ffn_bg1': (0.0, 0.8),
     'L0_ffn_bg2': (0.0, 0.401),
     'L0_ffn_bp': (0.0, 0.1)}
    factors = {'L0_gnn_Wq': 8.0,
     'L0_gnn_Wk': 8.0,
     'L0_gnn_bv': 6.338,
     'L0_gnn_bo': 3.002,
     'L0_ffn_Wqk': 8.0,
     'L0_ffn_Wv': 4.381,
     'L0_ffn_conv_w': 8.0,
     'L0_ffn_Wg1': 8.0,
     'L0_ffn_Wg2': 8.0,
     'L0_ffn_Wp': 2.741}
    for name, (base, spread) in spreads.items():
        noise = np.random.default_rng([zlib.crc32(name.encode()), seed]).standard_normal(out[name].shape)
        drawn = base * np.exp(spread * noise) if base else spread * noise
        out[name] = jnp.asarray(drawn.astype(out[name].dtype))
    for name, factor in factors.items():
        out[name] = (out[name] * factor).astype(out[name].dtype)
    return out
```

```python
from contextlib import ExitStack

import concourse.bass as bass
from concourse import mybir

P = 128
ALU = mybir.AluOpType
ACT = mybir.ActivationFunctionType
AXX = mybir.AxisListType.X
F32 = mybir.dt.float32
F32R = mybir.dt.float32r

NB, T, C = 128, 128, 384
GB = 4
NG = NB // GB
KC = C // P
NH, HD = 12, 32
HPC = P // HD
SLOT = [(h % HPC) * KC + h // HPC for h in range(NH)]
NE = 3
GH = 32
VG = C + GH
EPS = 1e-5
A_SCALE = float(C) ** -0.5
B_SCALE = float(P) ** -0.5
MASKED = 1.0e30

A_RING, B_RING = 5, 3

EVAC = {"hT": "dve", "qk": "act", "v": "dve", "score": "dve", "turn": "act", "mix": "dve", "proj": "dve"}
RING = {"A": A_RING, "B": B_RING}
ORDER_OF_STEPS = {
    "pe": """
        A.hT.0 A.hT.1 A.hT.2 A.qk.0 A.qk.1 A.qk.2 A.qk.3 A.qk.4 A.qk.5 A.v.0 A.score.0.0 A.score.0.1
        A.score.0.2 A.score.0.3 A.v.1 A.score.1.0 A.v.2 A.v.3 B.hT.0 A.score.1.1 B.hT.1 B.hT.2
        A.score.1.2 A.turn.0.0 A.score.1.3 B.qk.0 B.v.0 A.turn.0.1 A.turn.0.2 A.score.2.0 B.v.1
        B.v.2 A.score.2.1 A.score.2.2 A.mix.0 A.score.2.3 B.v.3 A.turn.1.0 B.qk.1 A.turn.1.1
        A.turn.1.2 A.score.3.0 A.score.3.1 A.score.3.2 B.qk.2 A.score.3.3 B.qk.3 A.mix.1 B.qk.4
        A.turn.2.0 B.qk.5 A.proj.0 B.score.0 A.turn.2.1 B.score.1 A.turn.2.2 A.proj.1 A.mix.2
        A.turn.3.0 B.turn.0 B.score.2 A.turn.3.1 B.mix.0 B.turn.1 B.score.3 A.turn.3.2 B.proj.0
        B.mix.1 A.mix.3 B.turn.2 A.proj.2 A.proj.3 B.mix.2 B.turn.3 B.proj.1 B.mix.3 B.proj.2
        B.proj.3
    """,
    "act": """
        A.hT.0 A.hT.1 A.hT.2 A.qk.0 A.qk.1 A.qk.2 A.qk.3 A.qk.4 A.qk.5 A.score.0.0 A.score.0.1
        A.score.0.2 A.score.0.3 B.hT.0 B.hT.1 B.hT.2 A.score.1.0 A.turn.0.0 B.qk.0 A.score.1.1
        A.turn.0.1 A.score.1.2 A.score.1.3 A.turn.0.2 A.score.2.0 A.mix.0 A.score.2.1 A.turn.1.0
        A.score.2.2 A.turn.1.1 B.gate.0 A.score.2.3 A.turn.1.2 A.score.3.0 B.qk.1 B.qk.2 A.score.3.1
        A.mix.1 B.qk.3 A.score.3.2 B.gate.1 B.qk.4 A.score.3.3 A.turn.2.0 B.qk.5 A.turn.2.1
        B.score.0 A.turn.2.2 B.score.1 A.turn.3.0 B.turn.0 A.turn.3.1 B.mix.0 B.score.2 A.mix.2
        B.turn.1 A.turn.3.2 B.score.3 B.mix.1 A.mix.3 B.turn.2 B.mix.2 B.turn.3 B.mix.3
    """,
    "dve": """
        A.hT.0 A.hT.1 A.hT.2 A.ln1 A.v.0 A.score.0.0 A.score.0.1 A.score.0.2 A.score.0.3 A.score.1.0
        A.norm.0 A.v.1 B.hT.0 A.v.2 B.hT.1 B.hT.2 A.score.1.1 A.v.3 A.score.1.2 A.score.1.3 B.v.0
        B.conv A.score.2.0 B.v.1 A.norm.1 A.score.2.1 A.score.2.2 B.v.2 A.mix.0 A.score.2.3 B.v.3
        B.gate.0 A.score.3.0 A.score.3.1 A.norm.2 B.gate.1 A.score.3.2 A.score.3.3 A.mix.1 B.gate.2
        A.norm.3 B.score.0 B.score.1 B.norm.0 A.proj.0 A.proj.1 B.norm.1 A.ln2.0 B.score.2 B.mix.0
        B.score.3 B.norm.2 A.mix.2 A.ln2.1 B.norm.3 A.mix.3 B.proj.0 B.mix.1 A.proj.2 A.ln2.2
        A.proj.3 B.mix.2 A.ln2.3 B.proj.1 B.mix.3 B.proj.2 B.proj.3
    """,
    "pool": """
        A.res A.norm.0 A.norm.1 A.ln1 B.res A.norm.2 A.norm.3 B.norm.0 B.norm.1 A.ln2.0 B.norm.2
        A.ln2.1 B.norm.3 A.ln2.2 A.ln2.3 A.adj
    """,
    "sp": """
        A.res A.adj B.proj.0 B.proj.1 B.proj.2 B.proj.3
    """,
}


def parse(text):
    steps = []
    for word in text.split():
        stage, kind, *at = word.split(".")
        steps.append((stage, kind, *([int(n) for n in at] + [0, 0])[:2]))
    return steps


ORDER = {e: parse(text) for e, text in ORDER_OF_STEPS.items()}
GATE_LINKS = 18


def count(group, per_group, k):
    if isinstance(group, int):
        return group * per_group + k
    i, off = group
    v = i if per_group == 1 else i * per_group
    k += off * per_group
    return v + k if k else v


def static_zero(group):
    return isinstance(group, int) and group == 0


def build(nc, x, adj, wq, wk, wv, wo, a_bv, a_bo, wqk, bqk, wv2, wg1, wp, b_bv, bg1, wg2, bg2, b_bp,
          conv_w, conv_b, out):
    with ExitStack() as ctx:
        def sb(name, shape, dt=F32):
            return ctx.enter_context(nc.sbuf_tensor(name, shape, dt))

        def sem(name):
            return ctx.enter_context(nc.semaphore(name))

        bank = {s: [ctx.enter_context(nc.psum_tensor(f"{s}_bank{k}", [P, 512], F32)) for k in range(RING[s])]
                for s in "AB"}

        def parts(name, n):
            return sb(f"{name}_hi", [P, KC, n], F32R), sb(f"{name}_lo", [P, KC, n], F32R)

        WQ, WK, WV, WO = (parts(n, C) for n in ("wq", "wk", "wv", "wo"))
        WQ2, WK2, WP = (parts(n, C) for n in ("wq2", "wk2", "wp"))
        WV2 = parts("wv2g", VG)
        ident = sb("ident", [P, P])
        later = sb("later", [P, P])
        half = sb("half", [P, GB])
        bv_row = sb("bv_row", [P, C])
        bo_row = sb("bo_row", [P, C])
        bvg_row = sb("bvg_row", [P, VG])
        bp_row = sb("bp_row", [P, C])
        bg2_row = sb("bg2_row", [P, NE])
        wg2_row = sb("wg2_row", [P, NE, GH])
        bqk_col = sb("bqk_col", [P, 2 * KC])
        bq_neg = sb("bq_neg", [P, KC])
        conv_in = sb("conv_in", [P, 4])
        conv_neg = sb("conv_neg", [P, 4])
        conv_b0 = sb("conv_b0", [P, 1])

        xin = sb("xin", [P, GB, C])
        xres = sb("xres", [P, GB, C])
        h1 = sb("h1", [P, GB, C])
        hT_hi = sb("hT_hi", [P, KC, GB * T], F32R)
        hT_lo = sb("hT_lo", [P, KC, GB * T], F32R)
        qT = sb("qT", [P, KC, GB * T])
        kT = sb("kT", [P, KC, GB * T])
        V = sb("V", [P, GB, C])
        S = [sb(f"S{k}", [P, NH, T]) for k in range(2)]
        PT = [sb(f"PT{k}", [P, HPC * T]) for k in range(KC)]
        oT_hi = [sb(f"oT_hi{k}", [P, KC, T], F32R) for k in range(2)]
        oT_lo = [sb(f"oT_lo{k}", [P, KC, T], F32R) for k in range(2)]
        adj2 = sb("adj2", [P, GB, T])
        bn1 = sb("bn1", [P, GB, 6])
        mv1 = sb("mv1", [P, GB, 2])
        ve1 = sb("ve1", [P, GB])
        rstd1 = sb("rstd1", [P, GB])
        smin = [sb(f"smin{k}", [P, NH]) for k in range(2)]
        smax = [sb(f"smax{k}", [P, NH]) for k in range(2)]
        ssum = [sb(f"ssum{k}", [P, NH]) for k in range(2)]
        live = [sb(f"live{k}", [P, NH]) for k in range(2)]
        live2 = [sb(f"live2{k}", [P, NH]) for k in range(2)]
        rinv = [sb(f"rinv{k}", [P, NH]) for k in range(2)]
        rowf = [sb(f"rowf{k}", [P, NH]) for k in range(2)]

        x1 = sb("x1", [P, GB, C])
        x1res = sb("x1res", [P, GB, C])
        h2 = sb("h2", [P, GB, C])
        q2 = sb("q2", [P, KC, GB * T])
        k2 = sb("k2", [P, KC, GB * T])
        q2raw = sb("q2raw", [P, GB * T])
        V2 = sb("V2", [P, GB, VG])
        S2 = [sb(f"S2{k}", [P, NE, T]) for k in range(2)]
        PT2 = [sb(f"PT2{k}", [P, NE * T]) for k in range(2)]
        yT_hi = [sb(f"yT_hi{k}", [P, KC, T], F32R) for k in range(2)]
        yT_lo = [sb(f"yT_lo{k}", [P, KC, T], F32R) for k in range(2)]
        bn2 = sb("bn2", [P, GB, 6])
        mv2 = sb("mv2", [P, GB, 2])
        ve2 = sb("ve2", [P, GB])
        rstd2 = sb("rstd2", [P, GB])
        s2min = [sb(f"s2min{k}", [P, NE]) for k in range(2)]
        s2sum = [sb(f"s2sum{k}", [P, NE]) for k in range(2)]
        r2inv = [sb(f"r2inv{k}", [P, NE]) for k in range(2)]
        row2f = [sb(f"row2f{k}", [P, NE]) for k in range(2)]
        g_hid = sb("g_hid", [P, GB, GH])
        g_prod = q2raw[:, 0:NE * GB * GH].rearrange("p (e b n) -> p e b n", e=NE, b=GB)
        g_tmp = [sb(f"g_tmp{k}", [P, NE, GB]) for k in range(9)]
        g_col = [sb(f"g_col{k}", [P, GB]) for k in range(7)]
        g_w = sb("g_w", [P, NE, GB])

        products = {"A": sem("a_products"), "B": sem("b_products")}
        evacuated = {(s, e): sem(f"{s.lower()}_{e}_evacuated") for s in "AB" for e in ("act", "dve")}
        hi_ready = {"A": sem("a_hi_ready"), "B": sem("b_hi_ready")}
        consts_loaded, raw_loaded = sem("consts_loaded"), sem("raw_loaded")
        consts_built, consts_zeroed = sem("consts_built"), sem("consts_zeroed")
        w_hi, w_lo, bias_scaled = sem("w_hi"), sem("w_lo"), sem("bias_scaled")
        x_loaded, adj_loaded, adj_scaled, stored = sem("x_loaded"), sem("adj_loaded"), sem("adj_scaled"), sem("stored")
        stats1, moments1, vareps1, rstd1_done, h1_ready = (sem(n) for n in (
            "stats1", "moments1", "vareps1", "rstd1_done", "h1_ready"))
        stats2, moments2, vareps2, rstd2_done, h2_ready = (sem(n) for n in (
            "stats2", "moments2", "vareps2", "rstd2_done", "h2_ready"))
        xres_ready, x1res_ready = sem("xres_ready"), sem("x1res_ready")
        biased, exped, guard, row_factor, normed = (sem(n) for n in (
            "biased", "exped", "guard", "row_factor", "normed"))
        raw_query, conv_step, exped2, sums_inverted2, row_factor2, normed2 = (sem(n) for n in (
            "raw_query", "conv_step", "exped2", "sums_inverted2", "row_factor2", "normed2"))
        passed = {nc.vector.engine: sem("dve_passed"), nc.gpsimd.engine: sem("pool_passed")}
        gate_step, gate_exp = sem("gate_step"), sem("gate_exp")

        jobs = {s: [x for x in ORDER["pe"] if x[0] == s] for s in "AB"}
        evacs = {(s, e): [x for x in ORDER[e] if x[0] == s and EVAC.get(x[1]) == e]
                 for s in "AB" for e in ("act", "dve")}

        def index(step):
            return jobs[step[0]].index(step)

        def bank_of(step):
            return bank[step[0]][index(step) % RING[step[0]]]

        def wait_products(eng, step, g):
            eng.wait_ge(products[step[0]], count(g, len(jobs[step[0]]), index(step) + 1))

        def wait_evacuated(eng, step, g):
            s, e = step[0], EVAC[step[1]]
            done = evacs[s, e]
            eng.wait_ge(evacuated[s, e], count(g, len(done), done.index(step) + 1))

        def wait_bank(eng, step, g):
            s, j = step[0], index(step) - RING[step[0]]
            if j < 0:
                if static_zero(g):
                    return
                g = g - 1 if isinstance(g, int) else (g[0], g[1] - 1)
                j += -(-len(jobs[s]) // RING[s]) * RING[s]
                if j >= len(jobs[s]):
                    j -= RING[s]
            wait_evacuated(eng, jobs[s][j], g)

        def apart(eng):
            eng.sem_inc(passed[eng.engine], 1)

        def following(g):
            return g + 1 if isinstance(g, int) else (g[0], g[1] + 1)

        def groups(eng, name, do):
            order = ORDER[name]
            for step in order:
                if step[0] == "A":
                    do(step, 0, False)
            for step in order:
                do(step, 1 if step[0] == "A" else 0, False)
            with eng.Fori(0, NG - 3) as i:
                for step in order:
                    do(step, (i, 2) if step[0] == "A" else (i, 1), False)
            for step in order:
                do(step, NG - 1 if step[0] == "A" else NG - 2, True)
            for step in order:
                if step[0] == "B":
                    do(step, NG - 1, True)

        def dram_group(t, g):
            if isinstance(g, int):
                return t[g * GB:(g + 1) * GB].rearrange("b t c -> t b c")
            i, off = g
            return t[bass.ds((i + off) * GB if off else i * GB, GB)].rearrange("b t c -> t b c")

        raw = [(wq, WQ, S[0], C), (wk, WK, S[1], C), (wv, WV, q2, C), (wo, WO, k2, C),
               (wqk[:, :, 0:C], WQ2, x1, C), (wqk[:, :, C:2 * C], WK2, x1res, C), (wp, WP, h2, C)]

        def staged(t, n):
            flat = t[:].rearrange("p a b -> p (a b)")
            return flat[:, 0:KC * n].rearrange("p (c n) -> p c n", c=KC)

        rows = [(a_bv, bv_row[:]), (a_bo, bo_row[:]), (b_bv, bvg_row[:, 0:C]), (bg1, bvg_row[:, C:VG]),
                (b_bp, bp_row[:]), (bg2, bg2_row[:])]

        block = ctx.enter_context(nc.Block())

        @block.sync
        def _(sp):
            sp.dma_start(xin[:], dram_group(x, 0)).then_inc(x_loaded, 16)
            sp.dma_start(adj2[:], dram_group(adj, 0)).then_inc(adj_loaded, 16)
            for src, _, stage, n in raw:
                sp.dma_start(staged(stage, n), src).then_inc(raw_loaded, 16)
            v2_raw = staged(V2, VG)
            sp.dma_start(v2_raw[:, :, 0:C], wv2).then_inc(raw_loaded, 16)
            sp.dma_start(v2_raw[:, :, C:VG], wg1).then_inc(raw_loaded, 16)
            for src, dst in rows:
                sp.dma_start(dst, src.unsqueeze(0).broadcast_to([P, dst.shape[1]])).then_inc(consts_loaded, 16)
            sp.dma_start(wg2_row[:], wg2.unsqueeze(0).broadcast_to([P, NE, GH])).then_inc(consts_loaded, 16)
            sp.dma_start(bqk_col[:], bqk).then_inc(consts_loaded, 16)
            sp.dma_start(conv_in[:, 0:3], conv_w).then_inc(consts_loaded, 16)
            sp.dma_start(conv_in[:, 3:4], conv_b).then_inc(consts_loaded, 16)

            def do(step, g, last):
                stage, kind, b, _ = step
                if (stage, kind) == ("A", "res") and not last:
                    sp.wait_ge(xres_ready, count(g, 1, 1))
                    sp.dma_start(xin[:], dram_group(x, following(g))).then_inc(x_loaded, 16)
                if (stage, kind) == ("A", "adj") and not last:
                    wait_evacuated(sp, ("A", "score", GB - 1, HPC - 1), g)
                    sp.dma_start(adj2[:], dram_group(adj, following(g))).then_inc(adj_loaded, 16)
                if (stage, kind) == ("B", "proj"):
                    wait_evacuated(sp, step, g)
                    if isinstance(g, int):
                        dst = out[g * GB + b]
                    else:
                        dst = out[bass.ds(g[0] * GB + (g[1] * GB + b), 1)].rearrange("b t c -> (b t) c")
                    sp.dma_start(dst, x1res[:, b, :]).then_inc(stored, 16)

            groups(sp, "sp", do)
            sp.wait_ge(stored, 16 * NB)

        @block.tensor
        def _(pe):
            pe.wait_ge(w_lo, 8)
            pe.wait_ge(consts_built, 1)

            def three_pass(dst, left, right):
                pairs = [(0, 0), (0, 1), (1, 0)]
                for c in range(KC):
                    for n, (a, b) in enumerate(pairs):
                        mm = nc.tensor.matmul(dst, left(c)[a], right(c)[b], start=(c == 0 and n == 0),
                                              stop=(c == KC - 1 and n == 2))
                return mm

            def tok(b):
                return slice(b * T, (b + 1) * T)

            def do(step, g, last):
                stage, kind, b, c = step
                if kind not in EVAC:
                    return
                A = stage == "A"
                wait_bank(pe, step, g)
                dst = bank_of(step)
                if kind == "hT":
                    if b == 0:
                        if A:
                            pe.wait_ge(h1_ready, count(g, 1, 1))
                        else:
                            pe.wait_ge(h2_ready, count(g, GB, GB))
                    h = h1 if A else h2
                    for n in range(GB):
                        mm = nc.tensor.transpose(dst[:, tok(n)], h[:, n, b * P:(b + 1) * P], ident[:])
                elif kind == "qk":
                    if b == 0:
                        wait_evacuated(pe, (stage, "hT", KC - 1, 0), g)
                    W = ((WQ, WK) if A else (WQ2, WK2))[b // KC]
                    m = b % KC
                    mm = three_pass(dst[:, :], lambda c: [w[:, c, m * P:(m + 1) * P] for w in W],
                                    lambda c: [h[:, c, :] for h in (hT_hi, hT_lo)])
                elif kind == "v":
                    if b == 0:
                        wait_evacuated(pe, (stage, "hT", KC - 1, 0), g)
                    W, n = (WV, C) if A else (WV2, VG)
                    mm = three_pass(dst[:, 0:n], lambda c: [h[:, c, tok(b)] for h in (hT_hi, hT_lo)],
                                    lambda c: [w[:, c, :] for w in W])
                elif kind == "score" and A:
                    if b == 0:
                        wait_evacuated(pe, ("A", "qk", 2 * KC - 1, 0), g)
                    r = slice(c * HD, (c + 1) * HD)
                    for k in range(KC):
                        mm = nc.tensor.matmul(dst[:, tok(k)], qT[r, k, tok(b)], kT[r, k, tok(b)],
                                              start=True, stop=True)
                elif kind == "score":
                    if b == 0:
                        wait_evacuated(pe, ("B", "qk", 2 * KC - 1, 0), g)
                        pe.wait_ge(conv_step, count(g, 2, 2))
                    for e in range(NE):
                        mm = nc.tensor.matmul(dst[:, tok(e)], q2[:, e, tok(b)], k2[:, e, tok(b)],
                                              start=True, stop=True)
                elif kind == "turn" and A:
                    pe.wait_ge(normed, count(g, GB * KC, b * KC + c + 1))
                    for j in range(HPC):
                        mm = nc.tensor.transpose(dst[:, tok(j)], S[b % 2][:, c * HPC + j, :], ident[:])
                elif kind == "turn":
                    pe.wait_ge(normed2, count(g, GB, b + 1))
                    for e in range(NE):
                        mm = nc.tensor.transpose(dst[:, tok(e)], S2[b % 2][:, e, :], ident[:])
                elif kind == "mix" and A:
                    wait_evacuated(pe, ("A", "v", b, 0), g)
                    wait_evacuated(pe, ("A", "turn", b, KC - 1), g)
                    for k in range(KC):
                        for j in range(HPC):
                            h = k * HPC + j
                            mm = nc.tensor.matmul(dst[j * HD:(j + 1) * HD, tok(k)], V[:, b, h * HD:(h + 1) * HD],
                                                  PT[SLOT[h] // HPC][:, tok(SLOT[h] % HPC)],
                                                  start=True, stop=True)
                elif kind == "mix":
                    wait_evacuated(pe, ("B", "v", b, 0), g)
                    wait_evacuated(pe, ("B", "turn", b, 0), g)
                    for e in range(NE):
                        mm = nc.tensor.matmul(dst[:, tok(e)], V2[:, b, e * P:(e + 1) * P], PT2[b % 2][:, tok(e)],
                                              start=True, stop=True)
                elif kind == "proj":
                    wait_evacuated(pe, (stage, "mix", b, 0), g)
                    L = (oT_hi[b % 2], oT_lo[b % 2]) if A else (yT_hi[b % 2], yT_lo[b % 2])
                    W = WO if A else WP
                    mm = three_pass(dst[:, 0:C], lambda c: [t[:, c, :] for t in L], lambda c: [w[:, c, :] for w in W])
                mm.then_inc(products[stage], 1)

            groups(pe, "pe", do)

        @block.scalar
        def _(act):
            act.wait_ge(raw_loaded, 16 * 9)
            for _, (hi, _), stage, n in raw:
                nc.scalar.activation(hi[:], staged(stage, n), ACT.Copy).then_inc(w_hi, 1)
            nc.scalar.activation(WV2[0][:], staged(V2, VG), ACT.Copy).then_inc(w_hi, 1)
            act.wait_ge(bias_scaled, 3)
            act.wait_ge(w_lo, 8)

            def do(step, g, last):
                stage, kind, b, c = step
                A = stage == "A"
                src = bank_of(step) if kind in EVAC else None
                if kind == "hT":
                    wait_products(act, step, g)
                    nc.scalar.activation(hT_hi[:, b, :], src[:, :], ACT.Copy).then_inc(hi_ready[stage], 1)
                elif kind == "qk" and A:
                    wait_products(act, step, g)
                    if b < KC:
                        ins = nc.scalar.activation(qT[:, b, :], src[:, :], ACT.Copy, scale=-A_SCALE)
                    else:
                        ins = nc.scalar.activation(kT[:, b - KC, :], src[:, :], ACT.Copy)
                    ins.then_inc(evacuated["A", "act"], 1)
                elif kind == "qk":
                    wait_products(act, step, g)
                    if b == 0:
                        nc.scalar.activation(q2raw[:], src[:, :], ACT.Identity, bias=bqk_col[:, 0:1])
                        ins = nc.scalar.activation(q2[:, 0, :], src[:, :], ACT.Identity, bias=conv_b0[:, 0:1],
                                                   scale=conv_neg[:, 1:2])
                    elif b < KC:
                        ins = nc.scalar.activation(q2[:, b, :], src[:, :], ACT.Identity, bias=bq_neg[:, b:b + 1],
                                                   scale=-B_SCALE)
                    else:
                        ins = nc.scalar.activation(k2[:, b - KC, :], src[:, :], ACT.Identity, bias=bqk_col[:, b:b + 1])
                    ins.then_inc(evacuated["B", "act"], 1)
                elif kind == "score" and A:
                    wait_evacuated(act, step, g)
                    for h in range(c * KC, (c + 1) * KC):
                        ins = nc.scalar.activation(S[b % 2][:, h, :], S[b % 2][:, h, :], ACT.Exp,
                                                   bias=smin[b % 2][:, h:h + 1], scale=-1.0,
                                                   accum_out=ssum[b % 2][:, h:h + 1])
                    if c == HPC - 1:
                        ins.then_inc(exped, 1)
                elif kind == "score":
                    wait_evacuated(act, step, g)
                    for e in range(NE):
                        ins = nc.scalar.activation(S2[b % 2][:, e, :], S2[b % 2][:, e, :], ACT.Exp,
                                                   bias=s2min[b % 2][:, e:e + 1], scale=-1.0,
                                                   accum_out=s2sum[b % 2][:, e:e + 1])
                    ins.then_inc(exped2, 1)
                elif kind == "turn":
                    wait_products(act, step, g)
                    dst = PT[c][:, :] if A else PT2[b % 2][:, :]
                    nc.scalar.activation(dst, src[:, 0:dst.shape[1]], ACT.Copy).then_inc(evacuated[stage, "act"], 1)
                elif kind == "mix":
                    wait_products(act, step, g)
                    hi = oT_hi[b % 2] if A else yT_hi[b % 2]
                    nc.scalar.activation(hi[:].rearrange("p c t -> p (c t)"), src[:, 0:C],
                                         ACT.Copy).then_inc(hi_ready[stage], 1)
                elif kind == "gate" and b < 2:
                    act.wait_ge(gate_step, count(g, GATE_LINKS, (6, 11)[b]))
                    nc.scalar.activation(g_tmp[(2, 5)[b]][:], g_tmp[(1, 4)[b]][:], ACT.Exp).then_inc(gate_exp, 1)

            groups(act, "act", do)

        @block.vector
        def _(dve):
            for n_done, (_, (hi, lo), stage, n) in enumerate(raw):
                dve.wait_ge(w_hi, n_done + 1)
                nc.vector.tensor_tensor(lo[:], staged(stage, n), hi[:].bitcast(F32), ALU.subtract).then_inc(w_lo, 1)
            dve.wait_ge(w_hi, 8)
            nc.vector.tensor_tensor(WV2[1][:], staged(V2, VG), WV2[0][:].bitcast(F32), ALU.subtract).then_inc(w_lo, 1)
            dve.wait_ge(consts_loaded, 16 * (len(rows) + 4))
            nc.vector.tensor_scalar(bq_neg[:], bqk_col[:, 0:KC], -B_SCALE, None, ALU.mult).then_inc(bias_scaled, 1)
            nc.vector.tensor_scalar(conv_neg[:], conv_in[:], -B_SCALE, None, ALU.mult).then_inc(bias_scaled, 1)
            dve.wait_ge(bias_scaled, 2)
            nc.vector.scalar_tensor_tensor(out=conv_b0[:], in0=bqk_col[:, 0:1], scalar=conv_neg[:, 1:2],
                                           in1=conv_neg[:, 3:4], op0=ALU.mult, op1=ALU.add).then_inc(bias_scaled, 1)
            dve.wait_ge(w_lo, 8)
            dve.wait_ge(consts_built, 1)

            def layernorm1(g):
                dve.wait_ge(x_loaded, count(g, 16, 16))
                for b in range(GB):
                    ins = nc.vector.bn_stats(bn1[:, b, :], xin[:, b, :])
                ins.then_inc(stats1, 1)
                dve.wait_ge(stats1, count(g, 1, 1))
                apart(dve)
                for b in range(GB):
                    ins = nc.vector.bn_aggr(mv1[:, b, :], bn1[:, b, :])
                ins.then_inc(moments1, 1)

            layernorm1(0)

            def gate(part, g):
                k = [(0, 6, 12)[part]]

                def link(ins):
                    ins.then_inc(gate_step, 1)
                    k[0] += 1
                    dve.wait_ge(gate_step, count(g, GATE_LINKS, k[0]))

                def over_e(t):
                    return t[:].rearrange("p e b -> p b e")

                def each_e(col):
                    return col[:].unsqueeze(1).broadcast_to([P, NE, GB])

                logit, shifted, e1, gates, d2, e2, above, lowest, sel = g_tmp
                lmax, esum, einv, gmax, gmin, wsum, winv = g_col
                v = nc.vector
                if part == 0:
                    wait_evacuated(dve, ("B", "v", GB - 1, 0), g)
                    link(v.tensor_scalar(g_hid[:], V2[:, :, C:VG], 0.0, None, ALU.max))
                    for e in range(NE):
                        ins = v.tensor_tensor(g_prod[:, e], g_hid[:],
                                              wg2_row[:, e, :].unsqueeze(1).broadcast_to([P, GB, GH]), ALU.mult)
                    link(ins)
                    link(v.tensor_reduce(sel[:], g_prod, AXX, ALU.add))
                    link(v.tensor_tensor(logit[:], sel[:], bg2_row[:].unsqueeze(2).broadcast_to([P, NE, GB]), ALU.add))
                    ins = v.tensor_reduce(lmax[:], over_e(logit), AXX, ALU.max)
                    link(ins)
                    v.tensor_tensor(shifted[:], logit[:], each_e(lmax), ALU.subtract).then_inc(gate_step, 1)
                elif part == 1:
                    dve.wait_ge(gate_exp, count(g, 2, 1))
                    link(v.tensor_reduce(esum[:], over_e(e1), AXX, ALU.add))
                    link(v.reciprocal(einv[:], esum[:]))
                    link(v.tensor_tensor(gates[:], e1[:], each_e(einv), ALU.mult))
                    v.tensor_reduce(gmin[:], over_e(gates), AXX, ALU.min)
                    link(v.tensor_reduce(gmax[:], over_e(gates), AXX, ALU.max))
                    v.tensor_tensor(d2[:], gates[:], each_e(gmax), ALU.subtract).then_inc(gate_step, 1)
                    v.tensor_tensor(above[:], gates[:], each_e(gmin), ALU.not_equal)
                    v.tensor_tensor(lowest[:], gates[:], each_e(gmin), ALU.is_equal).then_inc(gate_step, 1)
                else:
                    dve.wait_ge(gate_step, count(g, GATE_LINKS, 12))
                    v.tensor_copy(sel[:, 2, :], above[:, 2, :])
                    link(v.tensor_tensor(sel[:, 0:2, :], above[:, 0:2, :], lowest[:, 1:3, :], ALU.max))
                    link(v.tensor_tensor(sel[:, 0, :], sel[:, 0, :], lowest[:, 2, :], ALU.max))
                    dve.wait_ge(gate_exp, count(g, 2, 2))
                    link(v.tensor_tensor(gates[:], e2[:], sel[:], ALU.mult))
                    link(v.tensor_reduce(wsum[:], over_e(gates), AXX, ALU.add))
                    link(v.reciprocal(winv[:], wsum[:]))
                    link(v.tensor_tensor(g_w[:], gates[:], each_e(winv), ALU.mult))

            def do(step, g, last):
                stage, kind, b, c = step
                A = stage == "A"
                src = bank_of(step) if kind in EVAC else None
                freed = evacuated[stage, "dve"]
                if kind == "hT":
                    hi_n = KC + GB
                    dve.wait_ge(hi_ready[stage], count(g, hi_n, b + 1))
                    nc.vector.tensor_tensor(hT_lo[:, b, :], src[:, :], hT_hi[:, b, :].bitcast(F32),
                                            ALU.subtract).then_inc(freed, 1)
                elif kind == "mix":
                    dve.wait_ge(hi_ready[stage], count(g, KC + GB, KC + b + 1))
                    hi, lo = (oT_hi[b % 2], oT_lo[b % 2]) if A else (yT_hi[b % 2], yT_lo[b % 2])
                    nc.vector.tensor_tensor(lo[:].rearrange("p c t -> p (c t)"), src[:, 0:C],
                                            hi[:].rearrange("p c t -> p (c t)").bitcast(F32),
                                            ALU.subtract).then_inc(freed, 1)
                elif kind == "v":
                    wait_products(dve, step, g)
                    V_b, row = (V[:, b, :], bv_row) if A else (V2[:, b, :], bvg_row)
                    nc.vector.tensor_tensor(V_b, src[:, 0:row.shape[1]], row[:], ALU.add).then_inc(freed, 1)
                elif kind == "score" and A:
                    if b == 0 and c == 0:
                        dve.wait_ge(adj_scaled, count(g, 1, 1))
                    wait_products(dve, step, g)
                    apart(dve)
                    for j in range(KC):
                        h = c * KC + j
                        ins = nc.vector.tensor_tensor_reduce(
                            S[b % 2][:, h, :], src[:, j * T:(j + 1) * T], adj2[:, b, :], 1.0, 3.0e38,
                            ALU.add, ALU.min, smin[b % 2][:, h:h + 1])
                    ins.then_inc(biased, 1)
                    dve.wait_ge(biased, count(g, GB * HPC, b * HPC + c + 1))
                    hs = slice(c * KC, (c + 1) * KC)
                    nc.vector.tensor_reduce(smax[b % 2][:, hs], S[b % 2][:, hs, :], AXX, ALU.max).then_inc(freed, 1)
                elif kind == "score":
                    wait_products(dve, step, g)
                    apart(dve)
                    for e in range(NE):
                        ins = nc.vector.tensor_tensor_reduce(
                            S2[b % 2][:, e, :], src[:, e * T:(e + 1) * T], later[:], 1.0, 3.0e38,
                            ALU.add, ALU.min, s2min[b % 2][:, e:e + 1])
                    ins.then_inc(freed, 1)
                elif kind == "norm" and A:
                    k = b % 2
                    nc.vector.tensor_scalar(live[k][:], smin[k][:], 0.0, None, ALU.not_equal).then_inc(guard, 1)
                    dve.wait_ge(guard, count(g, 2 * GB, 2 * b + 1))
                    dve.wait_ge(exped, count(g, GB, b + 1))
                    nc.vector.reciprocal(rinv[k][:], ssum[k][:])
                    nc.vector.scalar_tensor_tensor(out=live2[k][:], in0=smax[k][:], scalar=0.0, in1=live[k][:],
                                                   op0=ALU.not_equal, op1=ALU.max).then_inc(guard, 1)
                    dve.wait_ge(guard, count(g, 2 * GB, 2 * b + 2))
                    nc.vector.tensor_tensor(rowf[k][:], rinv[k][:], live2[k][:], ALU.mult).then_inc(row_factor, 1)
                elif kind == "norm":
                    k = b % 2
                    dve.wait_ge(exped2, count(g, GB, b + 1))
                    nc.vector.reciprocal(r2inv[k][:], s2sum[k][:]).then_inc(sums_inverted2, 1)
                    dve.wait_ge(sums_inverted2, count(g, GB, b + 1))
                    dve.wait_ge(gate_step, count(g, GATE_LINKS, GATE_LINKS))
                    nc.vector.tensor_tensor(row2f[k][:], r2inv[k][:], g_w[:, :, b], ALU.mult).then_inc(row_factor2, 1)
                elif kind == "proj" and A:
                    wait_products(dve, step, g)
                    dve.wait_ge(xres_ready, count(g, 1, 1))
                    if not static_zero(g):
                        dve.wait_ge(x1res_ready, count(g, 1, 0))
                    nc.vector.tensor_tensor(x1[:, b, :], src[:, 0:C], xres[:, b, :], ALU.add).then_inc(freed, 1)
                elif kind == "proj":
                    wait_products(dve, step, g)
                    dve.wait_ge(x1res_ready, count(g, 1, 1))
                    nc.vector.tensor_tensor(x1res[:, b, :], src[:, 0:C], x1res[:, b, :], ALU.add).then_inc(freed, 1)
                elif kind == "ln2":
                    wait_evacuated(dve, ("A", "proj", b, 0), g)
                    nc.vector.bn_stats(bn2[:, b, :], x1[:, b, :]).then_inc(stats2, 1)
                    dve.wait_ge(stats2, count(g, GB, b + 1))
                    apart(dve)
                    nc.vector.bn_aggr(mv2[:, b, :], bn2[:, b, :]).then_inc(moments2, 1)
                elif kind == "ln1" and not last:
                    layernorm1(following(g))
                elif kind == "conv":
                    wait_evacuated(dve, ("B", "qk", 0, 0), g)
                    q = q2[:, 0, :].rearrange("p (b t) -> p b t", b=GB)
                    r = q2raw[:].rearrange("p (b t) -> p b t", b=GB)
                    nc.vector.scalar_tensor_tensor(out=q[:, :, 1:T], in0=r[:, :, 0:T - 1], scalar=conv_neg[:, 0:1],
                                                   in1=q[:, :, 1:T], op0=ALU.mult, op1=ALU.add).then_inc(conv_step, 1)
                    dve.wait_ge(conv_step, count(g, 2, 1))
                    nc.vector.scalar_tensor_tensor(out=q[:, :, 0:T - 1], in0=r[:, :, 1:T], scalar=conv_neg[:, 2:3],
                                                   in1=q[:, :, 0:T - 1], op0=ALU.mult, op1=ALU.add).then_inc(conv_step, 1)
                elif kind == "gate":
                    gate(b, g)

            groups(dve, "dve", do)

        @block.gpsimd
        def _(pool):
            nc.gpsimd.memset(ident[:], 0.0)
            nc.gpsimd.memset(half[:], -0.5)
            nc.gpsimd.memset(later[:], 0.0).then_inc(consts_zeroed, 1)
            pool.wait_ge(consts_zeroed, 1)
            nc.gpsimd.affine_select(out=later[:], in_=later[:], compare_op=ALU.is_ge, fill=MASKED, base=0,
                                    pattern=[[-1, P]], channel_multiplier=1)
            nc.gpsimd.affine_select(out=ident[:], in_=ident[:], compare_op=ALU.not_equal, fill=1.0, base=0,
                                    pattern=[[-1, P]], channel_multiplier=1).then_inc(consts_built, 1)
            pool.wait_ge(consts_built, 1)
            pool.wait_ge(consts_loaded, 16 * (len(rows) + 4))
            pool.wait_ge(w_lo, 8)

            def scale_adj(g):
                pool.wait_ge(adj_loaded, count(g, 16, 16))
                apart(pool)
                nc.gpsimd.tensor_scalar(adj2[:], adj2[:], -2.0, None, ALU.mult).then_inc(adj_scaled, 1)

            def layernorm1(g):
                pool.wait_ge(moments1, count(g, 1, 1))
                apart(pool)
                nc.gpsimd.tensor_scalar(ve1[:], mv1[:, :, 1], EPS, None, ALU.add).then_inc(vareps1, 1)
                pool.wait_ge(vareps1, count(g, 1, 1))
                nc.gpsimd.tensor_tensor(rstd1[:], ve1[:], half[:], ALU.pow).then_inc(rstd1_done, 1)
                pool.wait_ge(rstd1_done, count(g, 1, 1))
                apart(pool)
                for b in range(GB):
                    ins = nc.gpsimd.tensor_scalar(h1[:, b, :], xin[:, b, :], mv1[:, b, 0:1], rstd1[:, b:b + 1],
                                                  ALU.subtract, ALU.mult)
                ins.then_inc(h1_ready, 1)

            scale_adj(0)
            layernorm1(0)

            def do(step, g, last):
                stage, kind, b, c = step
                A = stage == "A"
                if kind == "res" and A:
                    if not static_zero(g):
                        before = g - 1 if isinstance(g, int) else (g[0], g[1] - 1)
                        wait_evacuated(pool, ("A", "proj", GB - 1, 0), before)
                    nc.gpsimd.tensor_tensor(xres[:], xin[:], bo_row[:].unsqueeze(1).broadcast_to([P, GB, C]),
                                            ALU.add).then_inc(xres_ready, 1)
                elif kind == "res":
                    wait_evacuated(pool, ("A", "proj", GB - 1, 0), g)
                    pool.wait_ge(moments2, count(g, GB, GB))
                    if not static_zero(g):
                        pool.wait_ge(stored, count(g, 16 * GB, 0))
                    nc.gpsimd.tensor_tensor(x1res[:], x1[:], bp_row[:].unsqueeze(1).broadcast_to([P, GB, C]),
                                            ALU.add).then_inc(x1res_ready, 1)
                elif kind == "norm" and A:
                    pool.wait_ge(row_factor, count(g, GB, b + 1))
                    for n in range(KC):
                        hs = slice(n * HPC, (n + 1) * HPC)
                        nc.gpsimd.tensor_tensor(S[b % 2][:, hs, :], S[b % 2][:, hs, :],
                                                rowf[b % 2][:, hs].unsqueeze(2).broadcast_to([P, HPC, T]),
                                                ALU.mult).then_inc(normed, 1)
                elif kind == "norm":
                    pool.wait_ge(row_factor2, count(g, GB, b + 1))
                    nc.gpsimd.tensor_tensor(S2[b % 2][:], S2[b % 2][:],
                                            row2f[b % 2][:].unsqueeze(2).broadcast_to([P, NE, T]),
                                            ALU.mult).then_inc(normed2, 1)
                elif kind == "ln2":
                    pool.wait_ge(moments2, count(g, GB, b + 1))
                    apart(pool)
                    nc.gpsimd.tensor_scalar(ve2[:, b:b + 1], mv2[:, b, 1:2], EPS, None, ALU.add).then_inc(vareps2, 1)
                    pool.wait_ge(vareps2, count(g, GB, b + 1))
                    nc.gpsimd.tensor_tensor(rstd2[:, b:b + 1], ve2[:, b:b + 1], half[:, 0:1],
                                            ALU.pow).then_inc(rstd2_done, 1)
                    pool.wait_ge(rstd2_done, count(g, GB, b + 1))
                    apart(pool)
                    nc.gpsimd.tensor_scalar(h2[:, b, :], x1[:, b, :], mv2[:, b, 0:1], rstd2[:, b:b + 1],
                                            ALU.subtract, ALU.mult).then_inc(h2_ready, 1)
                elif kind == "ln1" and not last:
                    wait_products(pool, ("A", "hT", KC - 1, 0), g)
                    layernorm1(following(g))
                elif kind == "adj" and not last:
                    scale_adj(following(g))

            groups(pool, "pool", do)


def kernel(**inputs):
    import numpy as np
    import concourse.bacc as bacc
    from concourse.bass_utils import run_bass_kernel_spmd

    def rows(w):
        w = np.asarray(w)
        return np.ascontiguousarray(w.reshape(w.shape[0] // P, P, w.shape[1]).transpose(1, 0, 2))

    def flat(name):
        return np.ascontiguousarray(np.asarray(inputs[name]).reshape(-1))

    a, f = "L0_gnn_", "L0_ffn_"
    wv2 = np.asarray(inputs[f + "Wv"]).transpose(1, 0, 2).reshape(C, C)
    arrays = {
        "x": np.ascontiguousarray(inputs["x"]),
        "adj": np.ascontiguousarray(inputs["adj"]),
        "wq": rows(np.asarray(inputs[a + "Wq"]).T),
        "wk": rows(np.asarray(inputs[a + "Wk"]).T),
        "wv": rows(np.asarray(inputs[a + "Wv"]).T),
        "wo": rows(np.asarray(inputs[a + "Wo"]).T),
        "a_bv": flat(a + "bv"),
        "a_bo": flat(a + "bo"),
        "wqk": rows(inputs[f + "Wqk"]),
        "bqk": np.ascontiguousarray(np.asarray(inputs[f + "bqk"]).reshape(2 * KC, P).T),
        "wv2": rows(wv2),
        "wg1": rows(inputs[f + "Wg1"]),
        "wp": rows(inputs[f + "Wp"]),
        "b_bv": flat(f + "bv"),
        "bg1": flat(f + "bg1"),
        "wg2": np.ascontiguousarray(np.asarray(inputs[f + "Wg2"]).T),
        "bg2": flat(f + "bg2"),
        "b_bp": flat(f + "bp"),
        "conv_w": np.ascontiguousarray(np.asarray(inputs[f + "conv_w"]).reshape(P, 3)),
        "conv_b": np.ascontiguousarray(np.asarray(inputs[f + "conv_b"]).reshape(P, 1)),
    }
    nc = bacc.Bacc("TRN2", target_bir_lowering=False, num_devices=1)
    aps = {n: nc.dram_tensor(f"in_{n}", v.shape, F32, kind="ExternalInput").ap() for n, v in arrays.items()}
    out = nc.dram_tensor("out", (NB, T, C), F32, kind="ExternalOutput").ap()
    build(nc, out=out, **aps)
    r = run_bass_kernel_spmd(nc, [{f"in_{n}": v for n, v in arrays.items()}], core_ids=[0])
    return r.results[0]["out"]
```

```python
from contextlib import ExitStack

import concourse.bass as bass
from concourse import mybir

P = 128
ALU = mybir.AluOpType
ACT = mybir.ActivationFunctionType
AXX = mybir.AxisListType.X
F32 = mybir.dt.float32
F32R = mybir.dt.float32r

NB, T, C = 128, 128, 384
GB = 4
NG = NB // GB
KC = C // P
NH, HD = 12, 32
HPC = P // HD
SLOT = [(h % HPC) * KC + h // HPC for h in range(NH)]
NE = 3
GH = 32
VG = C + GH
EPS = 1e-5
A_SCALE = float(C) ** -0.5
B_SCALE = float(P) ** -0.5
MASKED = 1.0e30

A_RING, B_RING = 5, 3

EVAC = {"hT": "dve", "qk": "act", "v": "dve", "score": "dve", "turn": "act", "mix": "dve", "proj": "dve"}
RING = {"A": A_RING, "B": B_RING}
ORDER_OF_STEPS = {
    "pe": """
        A.qk.0 A.qk.1 A.qk.2 A.qk.3 A.qk.4 A.qk.5 A.v.0 A.v.1 A.score.0.0 A.v.2 A.v.3 B.hT.0
        A.score.0.2 B.hT.1 B.hT.2 A.score.1.0 A.score.1.2 B.v.0 B.v.1 B.v.2 B.qk.0 A.turn.0.0
        A.turn.0.1 A.turn.0.2 B.qk.1 B.v.3 A.score.2.0 A.score.2.2 A.mix.0 A.turn.1.0 B.qk.2 B.qk.3
        B.qk.4 B.qk.5 A.turn.1.1 A.turn.1.2 B.score.0 B.score.1 A.score.3.0 A.score.3.2 A.mix.1
        A.proj.0 B.turn.0 B.score.2 A.turn.2.0 A.turn.2.1 B.mix.0 A.turn.2.2 A.proj.1 A.hT.0
        B.turn.1 B.score.3 A.hT.1 A.mix.2 A.turn.3.0 A.turn.3.1 A.turn.3.2 B.proj.0 A.hT.2 B.mix.1
        A.mix.3 A.proj.2 B.turn.2 A.proj.3 B.mix.2 B.turn.3 B.proj.1 B.mix.3 B.proj.2 B.proj.3
    """,
    "act": """
        A.qk.0 A.qk.1 A.qk.2 A.qk.3 A.qk.4 A.qk.5 A.score.0.0 B.hT.0 A.score.0.1 B.hT.1 B.hT.2
        A.score.0.2 A.score.0.3 A.score.1.0 A.score.1.1 A.score.1.2 B.qk.0 A.score.1.3 A.turn.0.0
        B.qk.1 A.turn.0.1 A.turn.0.2 A.score.2.0 A.mix.0 A.score.2.1 B.qk.2 A.score.2.2 B.gate.0
        B.qk.3 A.score.2.3 A.turn.1.0 B.qk.4 B.gate.1 B.qk.5 A.turn.1.1 B.score.0 A.turn.1.2
        B.score.1 A.score.3.0 A.mix.1 A.score.3.1 B.turn.0 A.score.3.2 A.score.3.3 A.turn.2.0
        A.turn.2.1 A.turn.2.2 B.mix.0 A.hT.0 B.score.2 A.hT.1 A.turn.3.0 A.mix.2 B.turn.1 A.turn.3.1
        A.turn.3.2 B.score.3 A.mix.3 A.hT.2 B.mix.1 B.turn.2 B.mix.2 B.turn.3 B.mix.3
    """,
    "dve": """
        A.v.0 A.ln1 A.v.1 A.score.0.0 A.score.0.1 A.v.2 A.v.3 B.hT.0 A.score.0.2 B.hT.1 B.hT.2
        A.score.0.3 A.score.1.0 B.v.0 A.score.1.1 A.norm.0 B.v.1 A.score.1.2 A.score.1.3 B.v.2
        A.norm.1 B.conv B.v.3 A.score.2.0 A.score.2.1 A.score.2.2 B.gate.0 A.score.2.3 B.gate.1
        A.mix.0 B.gate.2 B.score.0 A.norm.2 B.score.1 A.score.3.0 B.norm.0 A.score.3.1 A.score.3.2
        A.score.3.3 A.mix.1 A.proj.0 B.norm.1 B.score.2 A.norm.3 A.proj.1 A.ln2.0 B.mix.0 A.hT.0
        B.score.3 A.hT.1 A.mix.2 A.ln2.1 B.norm.2 A.mix.3 B.norm.3 A.proj.2 B.proj.0 A.hT.2 B.mix.1
        A.ln2.2 A.proj.3 B.mix.2 A.ln2.3 B.proj.1 B.mix.3 B.proj.2 B.proj.3
    """,
    "pool": """
        A.res A.norm.0 A.norm.1 B.res A.ln1 A.norm.2 B.norm.0 B.norm.1 A.norm.3 A.ln2.0 B.norm.2
        A.ln2.1 B.norm.3 A.adj A.ln2.2 A.ln2.3
    """,
    "sp": """
        A.res A.adj B.proj.0 B.proj.1 B.proj.2 B.proj.3
    """,
}


def parse(text):
    steps = []
    for word in text.split():
        stage, kind, *at = word.split(".")
        steps.append((stage, kind, *([int(n) for n in at] + [0, 0])[:2]))
    return steps


ORDER = {e: parse(text) for e, text in ORDER_OF_STEPS.items()}
GATE_LINKS = 18


def count(group, per_group, k):
    if isinstance(group, int):
        return group * per_group + k
    i, off = group
    v = i if per_group == 1 else i * per_group
    k += off * per_group
    return v + k if k else v


def static_zero(group):
    return isinstance(group, int) and group == 0


def build(nc, x, adj, wq, wk, wv, wo, a_bv, a_bo, wqk, bqk, wv2, wg1, wp, b_bv, bg1, wg2, bg2, b_bp,
          conv_w, conv_b, out):
    with ExitStack() as ctx:
        def sb(name, shape, dt=F32):
            return ctx.enter_context(nc.sbuf_tensor(name, shape, dt))

        def sem(name):
            return ctx.enter_context(nc.semaphore(name))

        bank = {s: [ctx.enter_context(nc.psum_tensor(f"{s}_bank{k}", [P, 512], F32)) for k in range(RING[s])]
                for s in "AB"}

        def parts(name, n):
            return sb(f"{name}_hi", [P, KC, n], F32R), sb(f"{name}_lo", [P, KC, n], F32R)

        WQ, WK, WV, WO = (parts(n, C) for n in ("wq", "wk", "wv", "wo"))
        WQ2, WK2, WP = (parts(n, C) for n in ("wq2", "wk2", "wp"))
        WV2 = parts("wv2g", VG)
        ident = sb("ident", [P, P])
        later = sb("later", [P, P])
        half = sb("half", [P, GB])
        bv_row = sb("bv_row", [P, C])
        bo_row = sb("bo_row", [P, C])
        bvg_row = sb("bvg_row", [P, VG])
        bp_row = sb("bp_row", [P, C])
        bg2_row = sb("bg2_row", [P, NE])
        wg2_row = sb("wg2_row", [P, NE, GH])
        bqk_col = sb("bqk_col", [P, 2 * KC])
        bq_neg = sb("bq_neg", [P, KC])
        conv_in = sb("conv_in", [P, 4])
        conv_neg = sb("conv_neg", [P, 4])
        conv_b0 = sb("conv_b0", [P, 1])

        xin = sb("xin", [P, GB, C])
        xres = sb("xres", [P, GB, C])
        h1 = sb("h1", [P, GB, C])
        hT_hi = sb("hT_hi", [P, KC, GB * T], F32R)
        hT_lo = sb("hT_lo", [P, KC, GB * T], F32R)
        qT = sb("qT", [P, KC, GB * T])
        kT = sb("kT", [P, KC, GB * T])
        V = sb("V", [P, GB, C])
        S = [sb(f"S{k}", [P, NH, T]) for k in range(2)]
        PT = [sb(f"PT{k}", [P, HPC * T]) for k in range(KC)]
        oT_hi = [sb(f"oT_hi{k}", [P, KC, T], F32R) for k in range(2)]
        oT_lo = [sb(f"oT_lo{k}", [P, KC, T], F32R) for k in range(2)]
        adj2 = sb("adj2", [P, GB, T])
        bn1 = sb("bn1", [P, GB, 6])
        mv1 = sb("mv1", [P, GB, 2])
        ve1 = sb("ve1", [P, GB])
        rstd1 = sb("rstd1", [P, GB])
        smin = [sb(f"smin{k}", [P, NH]) for k in range(2)]
        smax = [sb(f"smax{k}", [P, NH]) for k in range(2)]
        ssum = [sb(f"ssum{k}", [P, NH]) for k in range(2)]
        live = [sb(f"live{k}", [P, NH]) for k in range(2)]
        live2 = [sb(f"live2{k}", [P, NH]) for k in range(2)]
        rinv = [sb(f"rinv{k}", [P, NH]) for k in range(2)]
        rowf = [sb(f"rowf{k}", [P, NH]) for k in range(2)]

        x1 = sb("x1", [P, GB, C])
        x1res = sb("x1res", [P, GB, C])
        h2 = sb("h2", [P, GB, C])
        q2 = sb("q2", [P, KC, GB * T])
        k2 = sb("k2", [P, KC, GB * T])
        q2raw = sb("q2raw", [P, GB * T])
        V2 = sb("V2", [P, GB, VG])
        S2 = [sb(f"S2{k}", [P, NE, T]) for k in range(2)]
        PT2 = [sb(f"PT2{k}", [P, NE * T]) for k in range(2)]
        yT_hi = [sb(f"yT_hi{k}", [P, KC, T], F32R) for k in range(2)]
        yT_lo = [sb(f"yT_lo{k}", [P, KC, T], F32R) for k in range(2)]
        bn2 = sb("bn2", [P, GB, 6])
        mv2 = sb("mv2", [P, GB, 2])
        ve2 = sb("ve2", [P, GB])
        rstd2 = sb("rstd2", [P, GB])
        s2min = [sb(f"s2min{k}", [P, NE]) for k in range(2)]
        s2sum = [sb(f"s2sum{k}", [P, NE]) for k in range(2)]
        r2inv = [sb(f"r2inv{k}", [P, NE]) for k in range(2)]
        row2f = [sb(f"row2f{k}", [P, NE]) for k in range(2)]
        g_hid = sb("g_hid", [P, GB, GH])
        g_prod = q2raw[:, 0:NE * GB * GH].rearrange("p (e b n) -> p e b n", e=NE, b=GB)
        g_tmp = [sb(f"g_tmp{k}", [P, NE, GB]) for k in range(9)]
        g_col = [sb(f"g_col{k}", [P, GB]) for k in range(7)]
        g_w = sb("g_w", [P, NE, GB])

        products = {"A": sem("a_products"), "B": sem("b_products")}
        evacuated = {(s, e): sem(f"{s.lower()}_{e}_evacuated") for s in "AB" for e in ("act", "dve")}
        hi_ready = {"A": sem("a_hi_ready"), "B": sem("b_hi_ready")}
        turned1, hT_hi_ready, hT_lo_ready = sem("turned1"), sem("hT_hi_ready"), sem("hT_lo_ready")
        consts_loaded = sem("consts_loaded")
        raw_loaded = [sem(f"raw_loaded{n}") for n in range(8)]
        consts_built, consts_zeroed = sem("consts_built"), sem("consts_zeroed")
        w_hi, w_lo, bias_scaled = sem("w_hi"), sem("w_lo"), sem("bias_scaled")
        x_loaded, adj_loaded, adj_scaled, stored = sem("x_loaded"), sem("adj_loaded"), sem("adj_scaled"), sem("stored")
        stats1, moments1, vareps1, rstd1_done, h1_ready = (sem(n) for n in (
            "stats1", "moments1", "vareps1", "rstd1_done", "h1_ready"))
        stats2, moments2, vareps2, rstd2_done, h2_ready = (sem(n) for n in (
            "stats2", "moments2", "vareps2", "rstd2_done", "h2_ready"))
        xres_ready, x1res_ready = sem("xres_ready"), sem("x1res_ready")
        biased, exped, guard, row_factor, normed = (sem(n) for n in (
            "biased", "exped", "guard", "row_factor", "normed"))
        raw_query, conv_step, exped2, sums_inverted2, row_factor2, normed2 = (sem(n) for n in (
            "raw_query", "conv_step", "exped2", "sums_inverted2", "row_factor2", "normed2"))
        passed = {nc.vector.engine: sem("dve_passed"), nc.gpsimd.engine: sem("pool_passed")}
        gate_step, gate_exp = sem("gate_step"), sem("gate_exp")

        ring = {s: [] for s in "AB"}
        for step in ORDER["pe"]:
            ring[step[0]].append(step)
            if step[:2] == ("A", "score"):
                ring["A"].append((*step[:3], step[3] + 1))

        def ahead(step):
            return step[:2] == ("A", "hT")

        jobs = {s: [x for x in ring[s] if not ahead(x)] for s in "AB"}
        evacs = {(s, e): [x for x in ORDER[e] if x[0] == s and EVAC.get(x[1]) == e and not ahead(x)]
                 for s in "AB" for e in ("act", "dve")}

        def bank_of(step):
            return bank[step[0]][ring[step[0]].index(step) % RING[step[0]]]

        def wait_products(eng, step, g):
            if ahead(step):
                eng.wait_ge(turned1, count(g, KC, step[2] + 1))
            else:
                done = jobs[step[0]]
                eng.wait_ge(products[step[0]], count(g, len(done), done.index(step) + 1))

        def wait_evacuated(eng, step, g):
            if ahead(step):
                eng.wait_ge(hT_lo_ready, count(g, KC, step[2] + 1))
            else:
                s, e = step[0], EVAC[step[1]]
                done = evacs[s, e]
                eng.wait_ge(evacuated[s, e], count(g, len(done), done.index(step) + 1))

        def wait_bank(eng, step, g):
            s = step[0]
            r, n = ring[s], len(ring[s])
            j = r.index(step) - RING[s]
            while True:
                if j < 0:
                    if isinstance(g, int) and (g < 0 or s == "B" and g == 0):
                        return
                    g = before(g)
                    j += -(-n // RING[s]) * RING[s]
                if j < n and (g != -1 or ahead(r[j])) and (g != NG - 1 or not ahead(r[j])):
                    break
                j -= RING[s]
            wait_evacuated(eng, r[j], following(g) if ahead(r[j]) else g)

        def apart(eng):
            eng.sem_inc(passed[eng.engine], 1)

        def following(g):
            return g + 1 if isinstance(g, int) else (g[0], g[1] + 1)

        def before(g):
            return g - 1 if isinstance(g, int) else (g[0], g[1] - 1)

        def groups(eng, name, do):
            order = ORDER[name]
            for step in order:
                if ahead(step):
                    do(step, -1, False)
            for step in order:
                if step[0] == "A":
                    do(step, 0, False)
            for step in order:
                do(step, 1 if step[0] == "A" else 0, False)
            with eng.Fori(0, NG - 3) as i:
                for step in order:
                    do(step, (i, 2) if step[0] == "A" else (i, 1), False)
            for step in order:
                do(step, NG - 1 if step[0] == "A" else NG - 2, True)
            for step in order:
                if step[0] == "B":
                    do(step, NG - 1, True)

        def dram_group(t, g):
            if isinstance(g, int):
                return t[g * GB:(g + 1) * GB].rearrange("b t c -> t b c")
            i, off = g
            return t[bass.ds((i + off) * GB if off else i * GB, GB)].rearrange("b t c -> t b c")

        raw = [(wq, WQ, S[0], C), (wk, WK, S[1], C), (wv, WV, q2, C), (wo, WO, k2, C),
               (wqk[:, :, 0:C], WQ2, x1, C), (wqk[:, :, C:2 * C], WK2, x1res, C), (wp, WP, h2, C), (wv2, WV2, V2, VG)]
        A_RAW = 4

        def staged(t, n):
            flat = t[:].rearrange("p a b -> p (a b)")
            return flat[:, 0:KC * n].rearrange("p (c n) -> p c n", c=KC)

        rows = [(a_bv, bv_row[:]), (a_bo, bo_row[:]), (b_bv, bvg_row[:, 0:C]), (bg1, bvg_row[:, C:VG]),
                (b_bp, bp_row[:]), (bg2, bg2_row[:])]

        block = ctx.enter_context(nc.Block())

        @block.sync
        def _(sp):
            sp.dma_start(xin[:], dram_group(x, 0)).then_inc(x_loaded, 16)
            sp.dma_start(adj2[:], dram_group(adj, 0)).then_inc(adj_loaded, 16)

            def load_raw(n):
                src, _, stage, width = raw[n]
                if n < 7:
                    sp.dma_start(staged(stage, width), src).then_inc(raw_loaded[n], 16)
                else:
                    sp.dma_start(staged(stage, width)[:, :, 0:C], src).then_inc(raw_loaded[n], 16)
                    sp.dma_start(staged(stage, width)[:, :, C:VG], wg1).then_inc(raw_loaded[n], 16)

            for n in range(3):
                load_raw(n)
            for src, dst in rows:
                sp.dma_start(dst, src.unsqueeze(0).broadcast_to([P, dst.shape[1]])).then_inc(consts_loaded, 16)
            sp.dma_start(wg2_row[:], wg2.unsqueeze(0).broadcast_to([P, NE, GH])).then_inc(consts_loaded, 16)
            sp.dma_start(bqk_col[:], bqk).then_inc(consts_loaded, 16)
            sp.dma_start(conv_in[:, 0:3], conv_w).then_inc(consts_loaded, 16)
            sp.dma_start(conv_in[:, 3:4], conv_b).then_inc(consts_loaded, 16)
            for n in range(3, 8):
                load_raw(n)

            def do(step, g, last):
                stage, kind, b, _ = step
                if (stage, kind) == ("A", "res") and not last:
                    sp.wait_ge(xres_ready, count(g, 1, 1))
                    sp.dma_start(xin[:], dram_group(x, following(g))).then_inc(x_loaded, 16)
                if (stage, kind) == ("A", "adj") and not last:
                    wait_evacuated(sp, ("A", "score", GB - 1, HPC - 1), g)
                    sp.dma_start(adj2[:], dram_group(adj, following(g))).then_inc(adj_loaded, 16)
                if (stage, kind) == ("B", "proj"):
                    wait_evacuated(sp, step, g)
                    if isinstance(g, int):
                        dst = out[g * GB + b]
                    else:
                        dst = out[bass.ds(g[0] * GB + (g[1] * GB + b), 1)].rearrange("b t c -> (b t) c")
                    sp.dma_start(dst, x1res[:, b, :]).then_inc(stored, 16)

            groups(sp, "sp", do)
            sp.wait_ge(stored, 16 * NB)

        @block.tensor
        def _(pe):
            pe.wait_ge(consts_built, 1)

            def three_pass(dst, left, right):
                pairs = [(0, 0), (0, 1), (1, 0)]
                for c in range(KC):
                    for n, (a, b) in enumerate(pairs):
                        mm = nc.tensor.matmul(dst, left(c)[a], right(c)[b], start=(c == 0 and n == 0),
                                              stop=(c == KC - 1 and n == 2))
                return mm

            def tok(b):
                return slice(b * T, (b + 1) * T)

            def do(step, g, last):
                stage, kind, b, c = step
                if kind not in EVAC:
                    return
                A = stage == "A"
                if ahead(step) and last:
                    return
                wait_bank(pe, step, g)
                dst = bank_of(step)
                if kind == "hT":
                    if b == 0:
                        if A:
                            pe.wait_ge(h1_ready, count(following(g), 1, 1))
                        else:
                            pe.wait_ge(h2_ready, count(g, GB, GB))
                    h = h1 if A else h2
                    for n in range(GB):
                        mm = nc.tensor.transpose(dst[:, tok(n)], h[:, n, b * P:(b + 1) * P], ident[:])
                elif kind == "qk":
                    if b == 0:
                        wait_evacuated(pe, (stage, "hT", KC - 1, 0), g)
                    if static_zero(g) and b % KC == 0:
                        pe.wait_ge(w_lo, (1 if A else 5) + b // KC)
                    W = ((WQ, WK) if A else (WQ2, WK2))[b // KC]
                    m = b % KC
                    mm = three_pass(dst[:, :], lambda c: [w[:, c, m * P:(m + 1) * P] for w in W],
                                    lambda c: [h[:, c, :] for h in (hT_hi, hT_lo)])
                elif kind == "v":
                    if b == 0:
                        wait_evacuated(pe, (stage, "hT", KC - 1, 0), g)
                    if static_zero(g) and b == 0:
                        pe.wait_ge(w_lo, 3 if A else 8)
                    W, n = (WV, C) if A else (WV2, VG)
                    mm = three_pass(dst[:, 0:n], lambda c: [h[:, c, tok(b)] for h in (hT_hi, hT_lo)],
                                    lambda c: [w[:, c, :] for w in W])
                elif kind == "score" and A:
                    if b == 0:
                        wait_evacuated(pe, ("A", "qk", 2 * KC - 1, 0), g)
                    pair = [step, (stage, kind, b, c + 1)]
                    wait_bank(pe, pair[1], g)
                    for k in range(KC):
                        for one in pair:
                            r = slice(one[3] * HD, (one[3] + 1) * HD)
                            mm = nc.tensor.matmul(bank_of(one)[:, tok(k)], qT[r, k, tok(b)], kT[r, k, tok(b)],
                                                  start=True, stop=True)
                            if k == KC - 1 and one is step:
                                mm.then_inc(products["A"], 1)
                elif kind == "score":
                    if b == 0:
                        wait_evacuated(pe, ("B", "qk", 2 * KC - 1, 0), g)
                        pe.wait_ge(conv_step, count(g, 2, 2))
                    for e in range(NE):
                        mm = nc.tensor.matmul(dst[:, tok(e)], q2[:, e, tok(b)], k2[:, e, tok(b)],
                                              start=True, stop=True)
                elif kind == "turn" and A:
                    pe.wait_ge(normed, count(g, GB * KC, b * KC + c + 1))
                    for j in range(HPC):
                        mm = nc.tensor.transpose(dst[:, tok(j)], S[b % 2][:, c * HPC + j, :], ident[:])
                elif kind == "turn":
                    pe.wait_ge(normed2, count(g, GB, b + 1))
                    for e in range(NE):
                        mm = nc.tensor.transpose(dst[:, tok(e)], S2[b % 2][:, e, :], ident[:])
                elif kind == "mix" and A:
                    wait_evacuated(pe, ("A", "v", b, 0), g)
                    wait_evacuated(pe, ("A", "turn", b, KC - 1), g)
                    for k in range(KC):
                        for j in range(HPC):
                            h = k * HPC + j
                            mm = nc.tensor.matmul(dst[j * HD:(j + 1) * HD, tok(k)], V[:, b, h * HD:(h + 1) * HD],
                                                  PT[SLOT[h] // HPC][:, tok(SLOT[h] % HPC)],
                                                  start=True, stop=True)
                elif kind == "mix":
                    wait_evacuated(pe, ("B", "v", b, 0), g)
                    wait_evacuated(pe, ("B", "turn", b, 0), g)
                    for e in range(NE):
                        mm = nc.tensor.matmul(dst[:, tok(e)], V2[:, b, e * P:(e + 1) * P], PT2[b % 2][:, tok(e)],
                                              start=True, stop=True)
                elif kind == "proj":
                    wait_evacuated(pe, (stage, "mix", b, 0), g)
                    if static_zero(g) and b == 0:
                        pe.wait_ge(w_lo, 4 if A else 7)
                    L = (oT_hi[b % 2], oT_lo[b % 2]) if A else (yT_hi[b % 2], yT_lo[b % 2])
                    W = WO if A else WP
                    mm = three_pass(dst[:, 0:C], lambda c: [t[:, c, :] for t in L], lambda c: [w[:, c, :] for w in W])
                mm.then_inc(turned1 if ahead(step) else products[stage], 1)

            groups(pe, "pe", do)

        @block.scalar
        def _(act):
            def split_hi(n):
                _, (hi, _), stage, width = raw[n]
                act.wait_ge(raw_loaded[n], 32 if n == 7 else 16)
                nc.scalar.activation(hi[:], staged(stage, width), ACT.Copy).then_inc(w_hi, 1)

            for n in range(A_RAW):
                split_hi(n)

            def do(step, g, last):
                stage, kind, b, c = step
                A = stage == "A"
                src = bank_of(step) if kind in EVAC else None
                if kind == "hT":
                    if ahead(step):
                        if last:
                            return
                        g = following(g)
                    wait_products(act, step, g)
                    nc.scalar.activation(hT_hi[:, b, :], src[:, :], ACT.Copy)\
                        .then_inc(hT_hi_ready if A else hi_ready["B"], 1)
                    if ahead(step) and static_zero(g) and b == KC - 1:
                        for n in range(A_RAW, 8):
                            split_hi(n)
                        act.wait_ge(w_lo, 8)
                        act.wait_ge(bias_scaled, 3)
                elif kind == "qk" and A:
                    wait_products(act, step, g)
                    if b < KC:
                        ins = nc.scalar.activation(qT[:, b, :], src[:, :], ACT.Copy, scale=-A_SCALE)
                    else:
                        ins = nc.scalar.activation(kT[:, b - KC, :], src[:, :], ACT.Copy)
                    ins.then_inc(evacuated["A", "act"], 1)
                elif kind == "qk":
                    wait_products(act, step, g)
                    if b == 0:
                        nc.scalar.activation(q2raw[:], src[:, :], ACT.Identity, bias=bqk_col[:, 0:1])
                        ins = nc.scalar.activation(q2[:, 0, :], src[:, :], ACT.Identity, bias=conv_b0[:, 0:1],
                                                   scale=conv_neg[:, 1:2])
                    elif b < KC:
                        ins = nc.scalar.activation(q2[:, b, :], src[:, :], ACT.Identity, bias=bq_neg[:, b:b + 1],
                                                   scale=-B_SCALE)
                    else:
                        ins = nc.scalar.activation(k2[:, b - KC, :], src[:, :], ACT.Identity, bias=bqk_col[:, b:b + 1])
                    ins.then_inc(evacuated["B", "act"], 1)
                elif kind == "score" and A:
                    wait_evacuated(act, step, g)
                    for h in range(c * KC, (c + 1) * KC):
                        ins = nc.scalar.activation(S[b % 2][:, h, :], S[b % 2][:, h, :], ACT.Exp,
                                                   bias=smin[b % 2][:, h:h + 1], scale=-1.0,
                                                   accum_out=ssum[b % 2][:, h:h + 1])
                    if c == HPC - 1:
                        ins.then_inc(exped, 1)
                elif kind == "score":
                    wait_evacuated(act, step, g)
                    for e in range(NE):
                        ins = nc.scalar.activation(S2[b % 2][:, e, :], S2[b % 2][:, e, :], ACT.Exp,
                                                   bias=s2min[b % 2][:, e:e + 1], scale=-1.0,
                                                   accum_out=s2sum[b % 2][:, e:e + 1])
                    ins.then_inc(exped2, 1)
                elif kind == "turn":
                    wait_products(act, step, g)
                    dst = PT[c][:, :] if A else PT2[b % 2][:, :]
                    nc.scalar.activation(dst, src[:, 0:dst.shape[1]], ACT.Copy).then_inc(evacuated[stage, "act"], 1)
                elif kind == "mix":
                    wait_products(act, step, g)
                    hi = oT_hi[b % 2] if A else yT_hi[b % 2]
                    nc.scalar.activation(hi[:].rearrange("p c t -> p (c t)"), src[:, 0:C],
                                         ACT.Copy).then_inc(hi_ready[stage], 1)
                elif kind == "gate" and b < 2:
                    act.wait_ge(gate_step, count(g, GATE_LINKS, (6, 11)[b]))
                    nc.scalar.activation(g_tmp[(2, 5)[b]][:], g_tmp[(1, 4)[b]][:], ACT.Exp).then_inc(gate_exp, 1)

            groups(act, "act", do)

        @block.vector
        def _(dve):
            def split_lo(n):
                _, (hi, lo), stage, width = raw[n]
                dve.wait_ge(w_hi, n + 1)
                nc.vector.tensor_tensor(lo[:], staged(stage, width), hi[:].bitcast(F32), ALU.subtract).then_inc(w_lo, 1)


            def layernorm1(g):
                dve.wait_ge(x_loaded, count(g, 16, 16))
                for b in range(GB):
                    ins = nc.vector.bn_stats(bn1[:, b, :], xin[:, b, :])
                ins.then_inc(stats1, 1)
                dve.wait_ge(stats1, count(g, 1, 1))
                apart(dve)
                for b in range(GB):
                    ins = nc.vector.bn_aggr(mv1[:, b, :], bn1[:, b, :])
                ins.then_inc(moments1, 1)

            layernorm1(0)
            for n in range(A_RAW):
                split_lo(n)
            dve.wait_ge(consts_loaded, 16 * (len(rows) + 4))
            nc.vector.tensor_scalar(bq_neg[:], bqk_col[:, 0:KC], -B_SCALE, None, ALU.mult).then_inc(bias_scaled, 1)
            nc.vector.tensor_scalar(conv_neg[:], conv_in[:], -B_SCALE, None, ALU.mult).then_inc(bias_scaled, 1)
            dve.wait_ge(bias_scaled, 2)
            nc.vector.scalar_tensor_tensor(out=conv_b0[:], in0=bqk_col[:, 0:1], scalar=conv_neg[:, 1:2],
                                           in1=conv_neg[:, 3:4], op0=ALU.mult, op1=ALU.add).then_inc(bias_scaled, 1)

            def gate(part, g):
                k = [(0, 6, 12)[part]]

                def link(ins):
                    ins.then_inc(gate_step, 1)
                    k[0] += 1
                    dve.wait_ge(gate_step, count(g, GATE_LINKS, k[0]))

                def over_e(t):
                    return t[:].rearrange("p e b -> p b e")

                def each_e(col):
                    return col[:].unsqueeze(1).broadcast_to([P, NE, GB])

                logit, shifted, e1, gates, d2, e2, above, lowest, sel = g_tmp
                lmax, esum, einv, gmax, gmin, wsum, winv = g_col
                v = nc.vector
                if part == 0:
                    wait_evacuated(dve, ("B", "v", GB - 1, 0), g)
                    link(v.tensor_scalar(g_hid[:], V2[:, :, C:VG], 0.0, None, ALU.max))
                    for e in range(NE):
                        ins = v.tensor_tensor(g_prod[:, e], g_hid[:],
                                              wg2_row[:, e, :].unsqueeze(1).broadcast_to([P, GB, GH]), ALU.mult)
                    link(ins)
                    link(v.tensor_reduce(sel[:], g_prod, AXX, ALU.add))
                    link(v.tensor_tensor(logit[:], sel[:], bg2_row[:].unsqueeze(2).broadcast_to([P, NE, GB]), ALU.add))
                    ins = v.tensor_reduce(lmax[:], over_e(logit), AXX, ALU.max)
                    link(ins)
                    v.tensor_tensor(shifted[:], logit[:], each_e(lmax), ALU.subtract).then_inc(gate_step, 1)
                elif part == 1:
                    dve.wait_ge(gate_exp, count(g, 2, 1))
                    link(v.tensor_reduce(esum[:], over_e(e1), AXX, ALU.add))
                    link(v.reciprocal(einv[:], esum[:]))
                    link(v.tensor_tensor(gates[:], e1[:], each_e(einv), ALU.mult))
                    v.tensor_reduce(gmin[:], over_e(gates), AXX, ALU.min)
                    link(v.tensor_reduce(gmax[:], over_e(gates), AXX, ALU.max))
                    v.tensor_tensor(d2[:], gates[:], each_e(gmax), ALU.subtract).then_inc(gate_step, 1)
                    v.tensor_tensor(above[:], gates[:], each_e(gmin), ALU.not_equal)
                    v.tensor_tensor(lowest[:], gates[:], each_e(gmin), ALU.is_equal).then_inc(gate_step, 1)
                else:
                    dve.wait_ge(gate_step, count(g, GATE_LINKS, 12))
                    v.tensor_copy(sel[:, 2, :], above[:, 2, :])
                    link(v.tensor_tensor(sel[:, 0:2, :], above[:, 0:2, :], lowest[:, 1:3, :], ALU.max))
                    link(v.tensor_tensor(sel[:, 0, :], sel[:, 0, :], lowest[:, 2, :], ALU.max))
                    dve.wait_ge(gate_exp, count(g, 2, 2))
                    link(v.tensor_tensor(gates[:], e2[:], sel[:], ALU.mult))
                    link(v.tensor_reduce(wsum[:], over_e(gates), AXX, ALU.add))
                    link(v.reciprocal(winv[:], wsum[:]))
                    link(v.tensor_tensor(g_w[:], gates[:], each_e(winv), ALU.mult))

            def do(step, g, last):
                stage, kind, b, c = step
                A = stage == "A"
                src = bank_of(step) if kind in EVAC else None
                freed = evacuated[stage, "dve"]
                if kind == "hT":
                    if A:
                        if last:
                            return
                        dve.wait_ge(hT_hi_ready, count(following(g), KC, b + 1))
                    else:
                        dve.wait_ge(hi_ready["B"], count(g, KC + GB, b + 1))
                    nc.vector.tensor_tensor(hT_lo[:, b, :], src[:, :], hT_hi[:, b, :].bitcast(F32),
                                            ALU.subtract).then_inc(hT_lo_ready if A else freed, 1)
                    if g == -1 and b == KC - 1:
                        for n in range(A_RAW, 8):
                            split_lo(n)
                        dve.wait_ge(w_lo, 8)
                        dve.wait_ge(consts_built, 1)
                elif kind == "mix":
                    dve.wait_ge(hi_ready[stage], count(g, GB, b + 1) if A else count(g, KC + GB, KC + b + 1))
                    hi, lo = (oT_hi[b % 2], oT_lo[b % 2]) if A else (yT_hi[b % 2], yT_lo[b % 2])
                    nc.vector.tensor_tensor(lo[:].rearrange("p c t -> p (c t)"), src[:, 0:C],
                                            hi[:].rearrange("p c t -> p (c t)").bitcast(F32),
                                            ALU.subtract).then_inc(freed, 1)
                elif kind == "v":
                    wait_products(dve, step, g)
                    V_b, row = (V[:, b, :], bv_row) if A else (V2[:, b, :], bvg_row)
                    nc.vector.tensor_tensor(V_b, src[:, 0:row.shape[1]], row[:], ALU.add).then_inc(freed, 1)
                elif kind == "score" and A:
                    if b == 0 and c == 0:
                        dve.wait_ge(adj_scaled, count(g, 1, 1))
                    wait_products(dve, step, g)
                    apart(dve)
                    for j in range(KC):
                        h = c * KC + j
                        ins = nc.vector.tensor_tensor_reduce(
                            S[b % 2][:, h, :], src[:, j * T:(j + 1) * T], adj2[:, b, :], 1.0, 3.0e38,
                            ALU.add, ALU.min, smin[b % 2][:, h:h + 1])
                    ins.then_inc(biased, 1)
                    dve.wait_ge(biased, count(g, GB * HPC, b * HPC + c + 1))
                    hs = slice(c * KC, (c + 1) * KC)
                    nc.vector.tensor_reduce(smax[b % 2][:, hs], S[b % 2][:, hs, :], AXX, ALU.max).then_inc(freed, 1)
                elif kind == "score":
                    wait_products(dve, step, g)
                    apart(dve)
                    for e in range(NE):
                        ins = nc.vector.tensor_tensor_reduce(
                            S2[b % 2][:, e, :], src[:, e * T:(e + 1) * T], later[:], 1.0, 3.0e38,
                            ALU.add, ALU.min, s2min[b % 2][:, e:e + 1])
                    ins.then_inc(freed, 1)
                elif kind == "norm" and A:
                    k = b % 2
                    nc.vector.tensor_scalar(live[k][:], smin[k][:], 0.0, None, ALU.not_equal).then_inc(guard, 1)
                    dve.wait_ge(guard, count(g, 2 * GB, 2 * b + 1))
                    dve.wait_ge(exped, count(g, GB, b + 1))
                    nc.vector.reciprocal(rinv[k][:], ssum[k][:])
                    nc.vector.scalar_tensor_tensor(out=live2[k][:], in0=smax[k][:], scalar=0.0, in1=live[k][:],
                                                   op0=ALU.not_equal, op1=ALU.max).then_inc(guard, 1)
                    dve.wait_ge(guard, count(g, 2 * GB, 2 * b + 2))
                    nc.vector.tensor_tensor(rowf[k][:], rinv[k][:], live2[k][:], ALU.mult).then_inc(row_factor, 1)
                elif kind == "norm":
                    k = b % 2
                    dve.wait_ge(exped2, count(g, GB, b + 1))
                    nc.vector.reciprocal(r2inv[k][:], s2sum[k][:]).then_inc(sums_inverted2, 1)
                    dve.wait_ge(sums_inverted2, count(g, GB, b + 1))
                    dve.wait_ge(gate_step, count(g, GATE_LINKS, GATE_LINKS))
                    nc.vector.tensor_tensor(row2f[k][:], r2inv[k][:], g_w[:, :, b], ALU.mult).then_inc(row_factor2, 1)
                elif kind == "proj" and A:
                    wait_products(dve, step, g)
                    dve.wait_ge(xres_ready, count(g, 1, 1))
                    if not static_zero(g):
                        dve.wait_ge(x1res_ready, count(g, 1, 0))
                    nc.vector.tensor_tensor(x1[:, b, :], src[:, 0:C], xres[:, b, :], ALU.add).then_inc(freed, 1)
                elif kind == "proj":
                    wait_products(dve, step, g)
                    dve.wait_ge(x1res_ready, count(g, 1, 1))
                    nc.vector.tensor_tensor(x1res[:, b, :], src[:, 0:C], x1res[:, b, :], ALU.add).then_inc(freed, 1)
                elif kind == "ln2":
                    wait_evacuated(dve, ("A", "proj", b, 0), g)
                    nc.vector.bn_stats(bn2[:, b, :], x1[:, b, :]).then_inc(stats2, 1)
                    dve.wait_ge(stats2, count(g, GB, b + 1))
                    apart(dve)
                    nc.vector.bn_aggr(mv2[:, b, :], bn2[:, b, :]).then_inc(moments2, 1)
                elif kind == "ln1" and not last:
                    layernorm1(following(g))
                elif kind == "conv":
                    wait_evacuated(dve, ("B", "qk", 0, 0), g)
                    q = q2[:, 0, :].rearrange("p (b t) -> p b t", b=GB)
                    r = q2raw[:].rearrange("p (b t) -> p b t", b=GB)
                    nc.vector.scalar_tensor_tensor(out=q[:, :, 1:T], in0=r[:, :, 0:T - 1], scalar=conv_neg[:, 0:1],
                                                   in1=q[:, :, 1:T], op0=ALU.mult, op1=ALU.add).then_inc(conv_step, 1)
                    dve.wait_ge(conv_step, count(g, 2, 1))
                    nc.vector.scalar_tensor_tensor(out=q[:, :, 0:T - 1], in0=r[:, :, 1:T], scalar=conv_neg[:, 2:3],
                                                   in1=q[:, :, 0:T - 1], op0=ALU.mult, op1=ALU.add).then_inc(conv_step, 1)
                elif kind == "gate":
                    gate(b, g)

            groups(dve, "dve", do)

        @block.gpsimd
        def _(pool):
            nc.gpsimd.memset(ident[:], 0.0)
            nc.gpsimd.memset(half[:], -0.5)
            nc.gpsimd.memset(later[:], 0.0).then_inc(consts_zeroed, 1)
            pool.wait_ge(consts_zeroed, 1)
            nc.gpsimd.affine_select(out=later[:], in_=later[:], compare_op=ALU.is_ge, fill=MASKED, base=0,
                                    pattern=[[-1, P]], channel_multiplier=1)
            nc.gpsimd.affine_select(out=ident[:], in_=ident[:], compare_op=ALU.not_equal, fill=1.0, base=0,
                                    pattern=[[-1, P]], channel_multiplier=1).then_inc(consts_built, 1)
            pool.wait_ge(consts_built, 1)

            def scale_adj(g):
                pool.wait_ge(adj_loaded, count(g, 16, 16))
                apart(pool)
                nc.gpsimd.tensor_scalar(adj2[:], adj2[:], -2.0, None, ALU.mult).then_inc(adj_scaled, 1)

            def layernorm1(g):
                pool.wait_ge(moments1, count(g, 1, 1))
                apart(pool)
                nc.gpsimd.tensor_scalar(ve1[:], mv1[:, :, 1], EPS, None, ALU.add).then_inc(vareps1, 1)
                pool.wait_ge(vareps1, count(g, 1, 1))
                nc.gpsimd.tensor_tensor(rstd1[:], ve1[:], half[:], ALU.pow).then_inc(rstd1_done, 1)
                pool.wait_ge(rstd1_done, count(g, 1, 1))
                apart(pool)
                for b in range(GB):
                    ins = nc.gpsimd.tensor_scalar(h1[:, b, :], xin[:, b, :], mv1[:, b, 0:1], rstd1[:, b:b + 1],
                                                  ALU.subtract, ALU.mult)
                ins.then_inc(h1_ready, 1)

            layernorm1(0)
            scale_adj(0)
            pool.wait_ge(consts_loaded, 16 * (len(rows) + 4))
            pool.wait_ge(w_lo, 8)

            def do(step, g, last):
                stage, kind, b, c = step
                A = stage == "A"
                if kind == "res" and A:
                    if not static_zero(g):
                        wait_evacuated(pool, ("A", "proj", GB - 1, 0), before(g))
                    nc.gpsimd.tensor_tensor(xres[:], xin[:], bo_row[:].unsqueeze(1).broadcast_to([P, GB, C]),
                                            ALU.add).then_inc(xres_ready, 1)
                elif kind == "res":
                    wait_evacuated(pool, ("A", "proj", GB - 1, 0), g)
                    pool.wait_ge(moments2, count(g, GB, GB))
                    if not static_zero(g):
                        pool.wait_ge(stored, count(g, 16 * GB, 0))
                    nc.gpsimd.tensor_tensor(x1res[:], x1[:], bp_row[:].unsqueeze(1).broadcast_to([P, GB, C]),
                                            ALU.add).then_inc(x1res_ready, 1)
                elif kind == "norm" and A:
                    pool.wait_ge(row_factor, count(g, GB, b + 1))
                    for n in range(KC):
                        hs = slice(n * HPC, (n + 1) * HPC)
                        nc.gpsimd.tensor_tensor(S[b % 2][:, hs, :], S[b % 2][:, hs, :],
                                                rowf[b % 2][:, hs].unsqueeze(2).broadcast_to([P, HPC, T]),
                                                ALU.mult).then_inc(normed, 1)
                elif kind == "norm":
                    pool.wait_ge(row_factor2, count(g, GB, b + 1))
                    nc.gpsimd.tensor_tensor(S2[b % 2][:], S2[b % 2][:],
                                            row2f[b % 2][:].unsqueeze(2).broadcast_to([P, NE, T]),
                                            ALU.mult).then_inc(normed2, 1)
                elif kind == "ln2":
                    pool.wait_ge(moments2, count(g, GB, b + 1))
                    apart(pool)
                    nc.gpsimd.tensor_scalar(ve2[:, b:b + 1], mv2[:, b, 1:2], EPS, None, ALU.add).then_inc(vareps2, 1)
                    pool.wait_ge(vareps2, count(g, GB, b + 1))
                    nc.gpsimd.tensor_tensor(rstd2[:, b:b + 1], ve2[:, b:b + 1], half[:, 0:1],
                                            ALU.pow).then_inc(rstd2_done, 1)
                    pool.wait_ge(rstd2_done, count(g, GB, b + 1))
                    apart(pool)
                    nc.gpsimd.tensor_scalar(h2[:, b, :], x1[:, b, :], mv2[:, b, 0:1], rstd2[:, b:b + 1],
                                            ALU.subtract, ALU.mult).then_inc(h2_ready, 1)
                elif kind == "ln1" and not last:
                    wait_products(pool, ("A", "hT", KC - 1, 0), g)
                    layernorm1(following(g))
                elif kind == "adj" and not last:
                    scale_adj(following(g))

            groups(pool, "pool", do)


def kernel(**inputs):
    import numpy as np
    import concourse.bacc as bacc
    from concourse.bass_utils import run_bass_kernel_spmd

    def rows(w):
        w = np.asarray(w)
        return np.ascontiguousarray(w.reshape(w.shape[0] // P, P, w.shape[1]).transpose(1, 0, 2))

    def flat(name):
        return np.ascontiguousarray(np.asarray(inputs[name]).reshape(-1))

    a, f = "L0_gnn_", "L0_ffn_"
    wv2 = np.asarray(inputs[f + "Wv"]).transpose(1, 0, 2).reshape(C, C)
    arrays = {
        "x": np.ascontiguousarray(inputs["x"]),
        "adj": np.ascontiguousarray(inputs["adj"]),
        "wq": rows(np.asarray(inputs[a + "Wq"]).T),
        "wk": rows(np.asarray(inputs[a + "Wk"]).T),
        "wv": rows(np.asarray(inputs[a + "Wv"]).T),
        "wo": rows(np.asarray(inputs[a + "Wo"]).T),
        "a_bv": flat(a + "bv"),
        "a_bo": flat(a + "bo"),
        "wqk": rows(inputs[f + "Wqk"]),
        "bqk": np.ascontiguousarray(np.asarray(inputs[f + "bqk"]).reshape(2 * KC, P).T),
        "wv2": rows(wv2),
        "wg1": rows(inputs[f + "Wg1"]),
        "wp": rows(inputs[f + "Wp"]),
        "b_bv": flat(f + "bv"),
        "bg1": flat(f + "bg1"),
        "wg2": np.ascontiguousarray(np.asarray(inputs[f + "Wg2"]).T),
        "bg2": flat(f + "bg2"),
        "b_bp": flat(f + "bp"),
        "conv_w": np.ascontiguousarray(np.asarray(inputs[f + "conv_w"]).reshape(P, 3)),
        "conv_b": np.ascontiguousarray(np.asarray(inputs[f + "conv_b"]).reshape(P, 1)),
    }
    nc = bacc.Bacc("TRN2", target_bir_lowering=False, num_devices=1)
    aps = {n: nc.dram_tensor(f"in_{n}", v.shape, F32, kind="ExternalInput").ap() for n, v in arrays.items()}
    out = nc.dram_tensor("out", (NB, T, C), F32, kind="ExternalOutput").ap()
    build(nc, out=out, **aps)
    r = run_bass_kernel_spmd(nc, [{f"in_{n}": v for n, v in arrays.items()}], core_ids=[0])
    return r.results[0]["out"]
```

```python
from contextlib import ExitStack

import concourse.bass as bass
from concourse import mybir

P = 128
ALU = mybir.AluOpType
ACT = mybir.ActivationFunctionType
AXX = mybir.AxisListType.X
F32 = mybir.dt.float32
F32R = mybir.dt.float32r
F16 = mybir.dt.float16
I32 = mybir.dt.int32

NB, T, C = 128, 128, 384
GB = 4
NG = NB // GB
KC = C // P
NH, HD = 12, 32
HPC = P // HD
STACK = 3
NE = 3
GH = 32
VG = C + GH
EPS = 1e-5
H_SCALE = 2.0 ** 6
QK_SHIFT = 2.0 ** -13
EXP_BITS = 0x7F800000
EXP_ONE = 1 << 23
W_TOP = 13
TINY = 2.0 ** -40
A_SCALE = float(C) ** -0.5
B_SCALE = float(P) ** -0.5
MASKED = 1.0e30

A_RING, B_RING = 5, 3

EVAC = {"hT": "dve", "qk": "act", "v": "dve", "score": "dve", "turn": "act", "mix": "dve", "proj": "dve"}
RING = {"A": A_RING, "B": B_RING}
ORDER_OF_STEPS = {
    "pe": """
        A.v.0 A.score.0.0 A.v.1 A.score.0.1 A.score.0.2 A.v.2 A.v.3 B.hT.0 B.hT.1 B.hT.2 A.score.1.0
        A.score.1.1 A.score.1.2 B.v.0 B.qk.0 B.v.1 B.qk.1 A.turn.0.0 B.v.2 A.turn.0.1 A.turn.0.2
        A.score.2.0 B.qk.2 A.score.2.1 A.score.2.2 B.v.3 B.qk.3 A.mix.0 B.qk.4 B.qk.5 A.proj.0
        A.hT.0 A.hT.1 A.hT.2 A.turn.1.0 A.turn.1.1 B.score.0 A.turn.1.2 A.score.3.0 B.score.1
        A.score.3.1 A.qk.0 A.qk.1 A.score.3.2 A.qk.2 A.qk.3 A.qk.4 B.turn.0 B.score.2 A.mix.1
        A.turn.2.0 A.qk.5 B.mix.0 B.turn.1 A.turn.2.1 B.score.3 A.turn.2.2 A.proj.1 A.mix.2 B.proj.0
        A.turn.3.0 A.turn.3.1 A.turn.3.2 B.turn.2 A.proj.2 A.mix.3 B.mix.1 B.mix.2 B.turn.3 A.proj.3
        B.proj.1 B.mix.3 B.proj.2 B.proj.3
    """,
    "act": """
        A.score.0.0 B.hT.0 B.hT.1 B.hT.2 A.score.0.1 A.score.0.2 A.score.1.0 B.qk.0 A.score.1.1
        B.qk.1 A.turn.0.0 A.turn.0.1 B.qk.2 A.score.1.2 A.turn.0.2 B.qk.3 B.gate.0 A.mix.0
        A.score.2.0 B.qk.4 A.score.2.1 B.gate.1 B.qk.5 A.hT.0 A.hT.1 A.hT.2 A.turn.1.0 A.score.2.2
        A.turn.1.1 A.qk.0 A.turn.1.2 B.score.0 A.score.3.0 A.qk.1 A.qk.2 B.score.1 A.score.3.1
        A.qk.3 A.score.3.2 A.qk.4 B.turn.0 B.mix.0 A.mix.1 A.turn.2.0 A.qk.5 A.turn.2.1 A.turn.2.2
        B.score.2 A.mix.2 B.turn.1 B.score.3 A.turn.3.0 A.turn.3.1 A.turn.3.2 B.turn.2 A.mix.3
        B.mix.1 B.mix.2 B.turn.3 B.mix.3
    """,
    "dve": """
        A.v.0 A.score.0.0 A.score.0.1 A.score.0.2 A.v.1 B.hT.0 B.hT.1 B.hT.2 A.v.2 A.score.1.0 B.v.0
        A.norm.0 A.ln1 A.score.1.1 A.v.3 B.v.1 A.score.1.2 B.v.2 A.score.2.0 B.conv B.v.3 B.gate.0
        A.score.2.1 A.mix.0 B.gate.1 A.norm.1 A.score.2.2 A.proj.0 A.hT.0 A.hT.1 A.hT.2 B.gate.2
        A.score.3.0 B.score.0 B.score.1 A.score.3.1 A.qk.0 A.score.3.2 A.qk.1 A.qk.2 B.norm.0
        A.norm.2 A.ln2.0 B.norm.1 B.score.2 A.qk.3 A.norm.3 A.qk.4 A.mix.1 B.mix.0 A.qk.5 B.score.3
        B.norm.2 A.proj.1 A.mix.2 B.proj.0 A.ln2.1 B.norm.3 A.proj.2 A.ln2.2 A.mix.3 B.mix.1 B.mix.2
        A.proj.3 A.ln2.3 B.proj.1 B.mix.3 B.proj.2 B.proj.3
    """,
    "pool": """
        A.res A.norm.0 A.ln1 B.res A.norm.1 B.norm.0 A.norm.2 B.norm.1 A.norm.3 A.ln2.0 B.norm.2
        A.adj B.norm.3 A.ln2.1 A.ln2.2 A.ln2.3
    """,
    "sp": """
        A.res A.adj A.stack.0 A.stack.1 B.proj.0 B.proj.1 B.proj.2 B.proj.3
    """,
}


def parse(text):
    steps = []
    for word in text.split():
        stage, kind, *at = word.split(".")
        steps.append((stage, kind, *([int(n) for n in at] + [0, 0])[:2]))
    return steps


ORDER = {e: parse(text) for e, text in ORDER_OF_STEPS.items()}
GATE_LINKS = 18


def evac_engine(step):
    return "dve" if step[:2] == ("A", "qk") else EVAC.get(step[1])


def count(group, per_group, k):
    if isinstance(group, int):
        return group * per_group + k
    i, off = group
    v = i if per_group == 1 else i * per_group
    k += off * per_group
    return v + k if k else v


def static_zero(group):
    return isinstance(group, int) and group == 0


def build(nc, x, adj, wq, wk, wv, wo, a_bv, a_bo, wqk, bqk, wv2, wg1, wp, b_bv, bg1, wg2, bg2, b_bp,
          conv_w, conv_b, out):
    with ExitStack() as ctx:
        def sb(name, shape, dt=F32):
            return ctx.enter_context(nc.sbuf_tensor(name, shape, dt))

        def sem(name):
            return ctx.enter_context(nc.semaphore(name))

        bank = {s: [ctx.enter_context(nc.psum_tensor(f"{s}_bank{k}", [P, 512], F32)) for k in range(RING[s])]
                for s in "AB"}

        def parts(name, n, dt):
            return sb(f"{name}_hi", [P, KC, n], dt), sb(f"{name}_lo", [P, KC, n], dt)

        WQ, WK, WV, WQ2, WK2 = (parts(n, C, F16) for n in ("wq", "wk", "wv", "wq2", "wk2"))
        WO, WP = (parts(n, C, F32R) for n in ("wo", "wp"))
        WV2 = parts("wv2g", VG, F16)
        wmax, wtop, wscale, winv, hinv = (sb(n, [P, 6]) for n in ("wmax", "wtop", "wscale", "winv", "hinv"))
        wexp = sb("wexp", [P, 6], I32)
        s_unit = sb("s_unit", [P, 1])
        s_unit_neg = sb("s_unit_neg", [P, 1])
        adj_unit = sb("adj_unit", [P, 1])
        s_kk = sb("s_kk", [P, 1])
        q2_unit = sb("q2_unit", [P, 1])
        conv_mid = sb("conv_mid", [P, 1])
        ident = sb("ident", [P, P])
        later = sb("later", [P, P])
        half = sb("half", [P, GB])
        bv_row = sb("bv_row", [P, C])
        bo_row = sb("bo_row", [P, C])
        bvg_row = sb("bvg_row", [P, VG])
        bp_row = sb("bp_row", [P, C])
        bg2_row = sb("bg2_row", [P, NE])
        wg2_row = sb("wg2_row", [P, NE, GH])
        bqk_col = sb("bqk_col", [P, 2 * KC])
        bq_neg = sb("bq_neg", [P, KC])
        conv_in = sb("conv_in", [P, 4])
        conv_neg = sb("conv_neg", [P, 4])
        conv_b0 = sb("conv_b0", [P, 1])

        xin = sb("xin", [P, GB, C])
        xres = sb("xres", [P, GB, C])
        h1 = sb("h1", [P, GB, C])
        hT_hi = sb("hT_hi", [P, KC, GB * T], F16)
        hT_lo = sb("hT_lo", [P, KC, GB * T], F16)
        q_parts, k_parts = ([sb(f"{n}_{p}", [P, KC, GB * T], F16) for p in ("hi", "lo")] for n in "qk")
        Qs = sb("Qs", [STACK * HD, NH, GB * T], F16)
        Ks = sb("Ks", [STACK * HD, NH, GB * T], F16)
        V = sb("V", [P, GB, C])
        S = [sb(f"S{k}", [P, NH, T]) for k in range(2)]
        PT = [sb(f"PT{k}", [P, HPC * T]) for k in range(KC)]
        oT_hi = [sb(f"oT_hi{k}", [P, KC, T], F32R) for k in range(2)]
        oT_lo = [sb(f"oT_lo{k}", [P, KC, T], F32R) for k in range(2)]
        adj2 = sb("adj2", [P, GB, T])
        bn1 = sb("bn1", [P, GB, 6])
        mv1 = sb("mv1", [P, GB, 2])
        ve1 = sb("ve1", [P, GB])
        rstd1 = sb("rstd1", [P, GB])
        smin = [sb(f"smin{k}", [P, NH]) for k in range(2)]
        sbias = [sb(f"sbias{k}", [P, NH]) for k in range(2)]
        smax = [sb(f"smax{k}", [P, NH]) for k in range(2)]
        ssum = [sb(f"ssum{k}", [P, NH]) for k in range(2)]
        live = [sb(f"live{k}", [P, NH]) for k in range(2)]
        live2 = [sb(f"live2{k}", [P, NH]) for k in range(2)]
        rinv = [sb(f"rinv{k}", [P, NH]) for k in range(2)]
        rowf = [sb(f"rowf{k}", [P, NH]) for k in range(2)]

        x1 = sb("x1", [P, GB, C])
        x1res = sb("x1res", [P, GB, C])
        h2 = sb("h2", [P, GB, C])
        q2 = sb("q2", [P, KC, GB * T])
        k2 = sb("k2", [P, KC, GB * T])
        q2raw = sb("q2raw", [P, GB * T])
        V2 = sb("V2", [P, GB, VG])
        S2 = [sb(f"S2{k}", [P, NE, T]) for k in range(2)]
        PT2 = [sb(f"PT2{k}", [P, NE * T]) for k in range(2)]
        yT_hi = [sb(f"yT_hi{k}", [P, KC, T], F32R) for k in range(2)]
        yT_lo = [sb(f"yT_lo{k}", [P, KC, T], F32R) for k in range(2)]
        bn2 = sb("bn2", [P, GB, 6])
        mv2 = sb("mv2", [P, GB, 2])
        ve2 = sb("ve2", [P, GB])
        rstd2 = sb("rstd2", [P, GB])
        s2min = [sb(f"s2min{k}", [P, NE]) for k in range(2)]
        s2sum = [sb(f"s2sum{k}", [P, NE]) for k in range(2)]
        r2inv = [sb(f"r2inv{k}", [P, NE]) for k in range(2)]
        row2f = [sb(f"row2f{k}", [P, NE]) for k in range(2)]
        g_hid = sb("g_hid", [P, GB, GH])
        g_prod = q2raw[:, 0:NE * GB * GH].rearrange("p (e b n) -> p e b n", e=NE, b=GB)
        g_tmp = [sb(f"g_tmp{k}", [P, NE, GB]) for k in range(9)]
        g_col = [sb(f"g_col{k}", [P, GB]) for k in range(7)]
        g_w = sb("g_w", [P, NE, GB])

        products = {s: sem(f"{s.lower()}_products") for s in ("A", "ahead", "B")}
        evacuated = {(s, e): sem(f"{s.lower()}_{e}_evacuated") for s in ("A", "ahead", "B") for e in ("act", "dve")
                     if (s, e) != ("ahead", "act")}
        hi_ready = {s: sem(f"{s.lower()}_hi_ready") for s in ("A", "ahead", "B")}
        consts_loaded = sem("consts_loaded")
        raw_loaded = [sem(f"raw_loaded{n}") for n in range(8)]
        consts_built, consts_zeroed = sem("consts_built"), sem("consts_zeroed")
        maxima, tops, scale_step, scales_ready = (sem(n) for n in ("maxima", "tops", "scale_step", "scales_ready"))
        qs_stacked, ks_stacked = sem("qs_stacked"), sem("ks_stacked")
        w_hi, w_lo, bias_scaled = sem("w_hi"), sem("w_lo"), sem("bias_scaled")
        x_loaded, adj_loaded, adj_scaled, stored = sem("x_loaded"), sem("adj_loaded"), sem("adj_scaled"), sem("stored")
        stats1, moments1, vareps1, rstd1_done, h1_ready = (sem(n) for n in (
            "stats1", "moments1", "vareps1", "rstd1_done", "h1_ready"))
        stats2, moments2, vareps2, rstd2_done, h2_ready = (sem(n) for n in (
            "stats2", "moments2", "vareps2", "rstd2_done", "h2_ready"))
        xres_ready, x1res_ready = sem("xres_ready"), sem("x1res_ready")
        biased, exped, guard, row_factor, normed = (sem(n) for n in (
            "biased", "exped", "guard", "row_factor", "normed"))
        raw_query, conv_step, exped2, sums_inverted2, row_factor2, normed2 = (sem(n) for n in (
            "raw_query", "conv_step", "exped2", "sums_inverted2", "row_factor2", "normed2"))
        passed = {nc.vector.engine: sem("dve_passed"), nc.gpsimd.engine: sem("pool_passed")}
        gate_step, gate_exp = sem("gate_step"), sem("gate_exp")

        ring = {s: [] for s in "AB"}
        for step in ORDER["pe"]:
            ring[step[0]].append(step)

        def ahead(step):
            return step[0] == "A" and step[1] in ("hT", "qk", "stack")

        def counted(step):
            return "ahead" if ahead(step) else step[0]

        jobs = {s: [x for x in ORDER["pe"] if counted(x) == s] for s in products}
        evacs = {(s, e): [x for x in ORDER[e] if counted(x) == s and evac_engine(x) == e] for s, e in evacuated}
        splits = {s: [x for x in ORDER["act"] if counted(x) == s and
                      (x[1] in ("hT", "mix") or x[:2] == ("A", "qk"))] for s in hi_ready}

        def bank_of(step):
            return bank[step[0]][ring[step[0]].index(step) % RING[step[0]]]

        def wait_products(eng, step, g):
            done = jobs[counted(step)]
            eng.wait_ge(products[counted(step)], count(g, len(done), done.index(step) + 1))

        def wait_hi(eng, step, g):
            done = splits[counted(step)]
            eng.wait_ge(hi_ready[counted(step)], count(g, len(done), done.index(step) + 1))

        def wait_evacuated(eng, step, g):
            s, e = counted(step), evac_engine(step)
            done = evacs[s, e]
            eng.wait_ge(evacuated[s, e], count(g, len(done), done.index(step) + 1))

        def wait_bank(eng, step, g):
            s = step[0]
            r, n = ring[s], len(ring[s])
            j = r.index(step) - RING[s]
            while True:
                if j < 0:
                    if isinstance(g, int) and (g < 0 or s == "B" and g == 0):
                        return
                    g = before(g)
                    j += -(-n // RING[s]) * RING[s]
                if j < n and (g != -1 or ahead(r[j])) and (g != NG - 1 or not ahead(r[j])):
                    break
                j -= RING[s]
            wait_evacuated(eng, r[j], following(g) if ahead(r[j]) else g)

        def apart(eng):
            eng.sem_inc(passed[eng.engine], 1)

        def following(g):
            return g + 1 if isinstance(g, int) else (g[0], g[1] + 1)

        def before(g):
            return g - 1 if isinstance(g, int) else (g[0], g[1] - 1)

        def groups(eng, name, do):
            order = ORDER[name]

            def both(a, b, last):
                for step in order:
                    if ahead(step):
                        if not last:
                            do(step, following(a), False)
                    elif step[0] == "A":
                        do(step, a, last)
                    elif b is not None:
                        do(step, b, last)

            for step in order:
                if ahead(step):
                    do(step, 0, False)
            both(0, None, False)
            both(1, 0, False)
            with eng.Fori(0, NG - 3) as i:
                both((i, 2), (i, 1), False)
            both(NG - 1, NG - 2, True)
            for step in order:
                if step[0] == "B":
                    do(step, NG - 1, True)

        def dram_group(t, g):
            if isinstance(g, int):
                return t[g * GB:(g + 1) * GB].rearrange("b t c -> t b c")
            i, off = g
            return t[bass.ds((i + off) * GB if off else i * GB, GB)].rearrange("b t c -> t b c")

        raw = [(wq, WQ, S[0], C, 0), (wk, WK, S[1], C, 1), (wv, WV, q2, C, 2), (wo, WO, k2, C, None),
               (wqk[:, :, 0:C], WQ2, x1, C, 3), (wqk[:, :, C:2 * C], WK2, x1res, C, 4), (wp, WP, h2, C, None),
               (wv2, WV2, V2, VG, 5)]
        A_RAW = 4

        def staged(t, n):
            flat = t[:].rearrange("p a b -> p (a b)")
            return flat[:, 0:KC * n].rearrange("p (c n) -> p c n", c=KC)

        rows = [(a_bv, bv_row[:]), (a_bo, bo_row[:]), (b_bv, bvg_row[:, 0:C]), (bg1, bvg_row[:, C:VG]),
                (b_bp, bp_row[:]), (bg2, bg2_row[:])]

        block = ctx.enter_context(nc.Block())

        @block.sync
        def _(sp):
            sp.dma_start(xin[:], dram_group(x, 0)).then_inc(x_loaded, 16)
            sp.dma_start(adj2[:], dram_group(adj, 0)).then_inc(adj_loaded, 16)

            def load_raw(n):
                src, _, stage, width, _ = raw[n]
                if n < 7:
                    sp.dma_start(staged(stage, width), src).then_inc(raw_loaded[n], 16)
                else:
                    sp.dma_start(staged(stage, width)[:, :, 0:C], src).then_inc(raw_loaded[n], 16)
                    sp.dma_start(staged(stage, width)[:, :, C:VG], wg1).then_inc(raw_loaded[n], 16)

            for n in range(3):
                load_raw(n)
            for src, dst in rows:
                sp.dma_start(dst, src.unsqueeze(0).broadcast_to([P, dst.shape[1]])).then_inc(consts_loaded, 16)
            sp.dma_start(wg2_row[:], wg2.unsqueeze(0).broadcast_to([P, NE, GH])).then_inc(consts_loaded, 16)
            sp.dma_start(bqk_col[:], bqk).then_inc(consts_loaded, 16)
            sp.dma_start(conv_in[:, 0:3], conv_w).then_inc(consts_loaded, 16)
            sp.dma_start(conv_in[:, 3:4], conv_b).then_inc(consts_loaded, 16)
            for n in range(3, 8):
                load_raw(n)

            def do(step, g, last):
                stage, kind, b, _ = step
                if (stage, kind) == ("A", "res") and not last:
                    sp.wait_ge(xres_ready, count(g, 1, 1))
                    sp.dma_start(xin[:], dram_group(x, following(g))).then_inc(x_loaded, 16)
                if (stage, kind) == ("A", "stack"):
                    wait_evacuated(sp, ("A", "qk", (b + 1) * KC - 1, 0), g)
                    if not static_zero(g):
                        wait_products(sp, ("A", "score", GB - 1, KC - 1), before(g))
                    src, dst, done = ((q_parts, Qs, qs_stacked), (k_parts, Ks, ks_stacked))[b]
                    heads = dst[:].rearrange("p (c j) t -> p c j t", c=KC)
                    for n in range(STACK):
                        part = src[n // 2 if b == 0 else n % 2]
                        for j in range(HPC):
                            sp.dma_start(heads[n * HD:(n + 1) * HD, :, j, :],
                                         part[j * HD:(j + 1) * HD, :, :]).then_inc(done, 16)
                if (stage, kind) == ("A", "adj") and not last:
                    wait_evacuated(sp, ("A", "score", GB - 1, KC - 1), g)
                    sp.dma_start(adj2[:], dram_group(adj, following(g))).then_inc(adj_loaded, 16)
                if (stage, kind) == ("B", "proj"):
                    wait_evacuated(sp, step, g)
                    if isinstance(g, int):
                        dst = out[g * GB + b]
                    else:
                        dst = out[bass.ds(g[0] * GB + (g[1] * GB + b), 1)].rearrange("b t c -> (b t) c")
                    sp.dma_start(dst, x1res[:, b, :]).then_inc(stored, 16)

            groups(sp, "sp", do)
            sp.wait_ge(stored, 16 * NB)

        @block.tensor
        def _(pe):
            pe.wait_ge(consts_built, 1)

            def three_pass(dst, left, right):
                pairs = [(0, 0), (0, 1), (1, 0)]
                for c in range(KC):
                    for n, (a, b) in enumerate(pairs):
                        mm = nc.tensor.matmul(dst, left(c)[a], right(c)[b], start=(c == 0 and n == 0),
                                              stop=(c == KC - 1 and n == 2))
                return mm

            def tok(b):
                return slice(b * T, (b + 1) * T)

            def do(step, g, last):
                stage, kind, b, c = step
                if kind not in EVAC:
                    return
                A = stage == "A"
                wait_bank(pe, step, before(g) if ahead(step) else g)
                dst = bank_of(step)
                if kind == "hT":
                    if b == 0:
                        if A:
                            pe.wait_ge(h1_ready, count(g, 1, 1))
                        else:
                            pe.wait_ge(h2_ready, count(g, GB, GB))
                    h = h1 if A else h2
                    for n in range(GB):
                        mm = nc.tensor.transpose(dst[:, tok(n)], h[:, n, b * P:(b + 1) * P], ident[:])
                elif kind == "qk":
                    if b == 0:
                        wait_evacuated(pe, (stage, "hT", KC - 1, 0), g)
                    if static_zero(g) and b % KC == 0:
                        pe.wait_ge(w_lo, (1 if A else 5) + b // KC)
                    W = ((WQ, WK) if A else (WQ2, WK2))[b // KC]
                    m = b % KC
                    mm = three_pass(dst[:, :], lambda c: [w[:, c, m * P:(m + 1) * P] for w in W],
                                    lambda c: [h[:, c, :] for h in (hT_hi, hT_lo)])
                elif kind == "v":
                    if b == 0:
                        wait_evacuated(pe, (stage, "hT", KC - 1, 0), g)
                    if static_zero(g) and b == 0:
                        pe.wait_ge(w_lo, 3 if A else 8)
                    W, n = (WV, C) if A else (WV2, VG)
                    mm = three_pass(dst[:, 0:n], lambda c: [h[:, c, tok(b)] for h in (hT_hi, hT_lo)],
                                    lambda c: [w[:, c, :] for w in W])
                elif kind == "score" and A:
                    if b == 0 and c == 0:
                        for stacked in (qs_stacked, ks_stacked):
                            pe.wait_ge(stacked, count(g, 16 * STACK * HPC, 16 * STACK * HPC))
                    for j in range(HPC):
                        mm = nc.tensor.matmul(dst[:, tok(j)], Qs[:, c * HPC + j, tok(b)], Ks[:, c * HPC + j, tok(b)],
                                              start=True, stop=True)
                elif kind == "score":
                    if b == 0:
                        wait_evacuated(pe, ("B", "qk", 2 * KC - 1, 0), g)
                        pe.wait_ge(conv_step, count(g, 2, 2))
                    for e in range(NE):
                        mm = nc.tensor.matmul(dst[:, tok(e)], q2[:, e, tok(b)], k2[:, e, tok(b)],
                                              start=True, stop=True)
                elif kind == "turn" and A:
                    pe.wait_ge(normed, count(g, GB * KC, b * KC + c + 1))
                    for j in range(HPC):
                        mm = nc.tensor.transpose(dst[:, tok(j)], S[b % 2][:, c * HPC + j, :], ident[:])
                elif kind == "turn":
                    pe.wait_ge(normed2, count(g, GB, b + 1))
                    for e in range(NE):
                        mm = nc.tensor.transpose(dst[:, tok(e)], S2[b % 2][:, e, :], ident[:])
                elif kind == "mix" and A:
                    wait_evacuated(pe, ("A", "v", b, 0), g)
                    wait_evacuated(pe, ("A", "turn", b, KC - 1), g)
                    for k in range(KC):
                        for j in range(HPC):
                            h = k * HPC + j
                            mm = nc.tensor.matmul(dst[j * HD:(j + 1) * HD, tok(k)], V[:, b, h * HD:(h + 1) * HD],
                                                  PT[k][:, tok(j)],
                                                  start=True, stop=True)
                elif kind == "mix":
                    wait_evacuated(pe, ("B", "v", b, 0), g)
                    wait_evacuated(pe, ("B", "turn", b, 0), g)
                    for e in range(NE):
                        mm = nc.tensor.matmul(dst[:, tok(e)], V2[:, b, e * P:(e + 1) * P], PT2[b % 2][:, tok(e)],
                                              start=True, stop=True)
                elif kind == "proj":
                    wait_evacuated(pe, (stage, "mix", b, 0), g)
                    if static_zero(g) and b == 0:
                        pe.wait_ge(w_lo, 4 if A else 7)
                    L = (oT_hi[b % 2], oT_lo[b % 2]) if A else (yT_hi[b % 2], yT_lo[b % 2])
                    W = WO if A else WP
                    mm = three_pass(dst[:, 0:C], lambda c: [t[:, c, :] for t in L], lambda c: [w[:, c, :] for w in W])
                mm.then_inc(products[counted(step)], 1)

            groups(pe, "pe", do)

        @block.scalar
        def _(act):
            def split_hi(n):
                _, (hi, _), stage, width, col = raw[n]
                act.wait_ge(raw_loaded[n], 32 if n == 7 else 16)
                if col is None:
                    ins = nc.scalar.activation(hi[:], staged(stage, width), ACT.Copy)
                else:
                    act.wait_ge(scales_ready, 1 + col // 3)
                    ins = nc.scalar.activation(hi[:], staged(stage, width), ACT.Copy, scale=wscale[:, col:col + 1])
                ins.then_inc(w_hi, 1)

            for n in range(A_RAW):
                split_hi(n)

            def do(step, g, last):
                stage, kind, b, c = step
                A = stage == "A"
                src = bank_of(step) if kind in EVAC else None
                if kind == "hT":
                    wait_products(act, step, g)
                    nc.scalar.activation(hT_hi[:, b, :], src[:, :], ACT.Copy, scale=H_SCALE)\
                        .then_inc(hi_ready[counted(step)], 1)
                elif kind == "qk" and A:
                    wait_products(act, step, g)
                    if not static_zero(g):
                        act.wait_ge((qs_stacked, ks_stacked)[b // KC], count(g, 16 * STACK * HPC, 0))
                    dst = (q_parts, k_parts)[b // KC][0][:, b % KC, :]
                    nc.scalar.activation(dst, src[:, :], ACT.Copy,
                                         scale=-QK_SHIFT if b < KC else QK_SHIFT).then_inc(hi_ready["ahead"], 1)
                    if static_zero(g) and b == 2 * KC - 1:
                        for n in range(A_RAW, 8):
                            split_hi(n)
                        act.wait_ge(w_lo, 8)
                        act.wait_ge(bias_scaled, 4)
                elif kind == "qk":
                    wait_products(act, step, g)
                    if b == 0:
                        nc.scalar.activation(q2raw[:], src[:, :], ACT.Identity, bias=bqk_col[:, 0:1],
                                             scale=hinv[:, 3:4])
                        ins = nc.scalar.activation(q2[:, 0, :], src[:, :], ACT.Identity, bias=conv_b0[:, 0:1],
                                                   scale=conv_mid[:])
                    elif b < KC:
                        ins = nc.scalar.activation(q2[:, b, :], src[:, :], ACT.Identity, bias=bq_neg[:, b:b + 1],
                                                   scale=q2_unit[:])
                    else:
                        ins = nc.scalar.activation(k2[:, b - KC, :], src[:, :], ACT.Identity, bias=bqk_col[:, b:b + 1],
                                                   scale=hinv[:, 4:5])
                    ins.then_inc(evacuated["B", "act"], 1)
                elif kind == "score" and A:
                    wait_evacuated(act, step, g)
                    for h in range(c * HPC, (c + 1) * HPC):
                        ins = nc.scalar.activation(S[b % 2][:, h, :], S[b % 2][:, h, :], ACT.Exp,
                                                   bias=sbias[b % 2][:, h:h + 1], scale=s_unit_neg[:],
                                                   accum_out=ssum[b % 2][:, h:h + 1])
                    if c == KC - 1:
                        ins.then_inc(exped, 1)
                elif kind == "score":
                    wait_evacuated(act, step, g)
                    for e in range(NE):
                        ins = nc.scalar.activation(S2[b % 2][:, e, :], S2[b % 2][:, e, :], ACT.Exp,
                                                   bias=s2min[b % 2][:, e:e + 1], scale=-1.0,
                                                   accum_out=s2sum[b % 2][:, e:e + 1])
                    ins.then_inc(exped2, 1)
                elif kind == "turn":
                    wait_products(act, step, g)
                    dst = PT[c][:, :] if A else PT2[b % 2][:, :]
                    nc.scalar.activation(dst, src[:, 0:dst.shape[1]], ACT.Copy).then_inc(evacuated[stage, "act"], 1)
                elif kind == "mix":
                    wait_products(act, step, g)
                    hi = oT_hi[b % 2] if A else yT_hi[b % 2]
                    nc.scalar.activation(hi[:].rearrange("p c t -> p (c t)"), src[:, 0:C],
                                         ACT.Copy).then_inc(hi_ready[stage], 1)
                elif kind == "gate" and b < 2:
                    act.wait_ge(gate_step, count(g, GATE_LINKS, (6, 11)[b]))
                    nc.scalar.activation(g_tmp[(2, 5)[b]][:], g_tmp[(1, 4)[b]][:], ACT.Exp).then_inc(gate_exp, 1)

            groups(act, "act", do)

        @block.vector
        def _(dve):
            def split_lo(n):
                _, (hi, lo), stage, width, col = raw[n]
                dve.wait_ge(w_hi, n + 1)
                if col is None:
                    ins = nc.vector.tensor_tensor(lo[:], staged(stage, width), hi[:].bitcast(F32), ALU.subtract)
                else:
                    ins = nc.vector.scalar_tensor_tensor(out=lo[:], in0=staged(stage, width),
                                                         scalar=wscale[:, col:col + 1], in1=hi[:],
                                                         op0=ALU.mult, op1=ALU.subtract)
                ins.then_inc(w_lo, 1)

            k_scale = [0]

            def link_scale(ins):
                ins.then_inc(scale_step, 1)
                k_scale[0] += 1
                dve.wait_ge(scale_step, k_scale[0])

            def weight_scales(half_of):
                cols = slice(3 * half_of, 3 * half_of + 3)
                for n, (_, _, stage, width, col) in enumerate(raw):
                    if col is not None and col // 3 == half_of:
                        dve.wait_ge(raw_loaded[n], 32 if n == 7 else 16)
                        ins = nc.vector.tensor_reduce(wmax[:, col:col + 1], staged(stage, width), mybir.AxisListType.XY,
                                                      ALU.max, apply_absolute_value=True)
                ins.then_inc(maxima, 1)
                dve.wait_ge(tops, half_of + 1)
                link_scale(nc.vector.tensor_scalar(wtop[:, cols], wtop[:, cols], TINY, None, ALU.max))
                link_scale(nc.vector.tensor_scalar(wexp[:, cols], wtop[:, cols].bitcast(I32), EXP_BITS, None,
                                                   ALU.bitwise_and))
                link_scale(nc.vector.tensor_scalar(wscale[:, cols].bitcast(I32), wexp[:, cols], -1.0,
                                                   float((254 + W_TOP) * EXP_ONE), ALU.mult, ALU.add))
                link_scale(nc.vector.tensor_scalar(winv[:, cols].bitcast(I32), wscale[:, cols].bitcast(I32), -1.0,
                                                   float(254 * EXP_ONE), ALU.mult, ALU.add))
                link_scale(nc.vector.tensor_scalar(hinv[:, cols], winv[:, cols], 1.0 / H_SCALE, None, ALU.mult))
                if half_of == 0:
                    link_scale(nc.vector.tensor_tensor(s_kk[:], hinv[:, 0:1], hinv[:, 1:2], ALU.mult))
                    link_scale(nc.vector.tensor_scalar(s_unit[:], s_kk[:], A_SCALE / QK_SHIFT ** 2, None, ALU.mult))
                    link_scale(nc.vector.tensor_scalar(s_unit_neg[:], s_unit[:], -1.0, None, ALU.mult))
                    link_scale(nc.vector.reciprocal(s_kk[:], s_unit[:]))
                    ins = nc.vector.tensor_scalar(adj_unit[:], s_kk[:], -2.0, None, ALU.mult)
                else:
                    ins = nc.vector.tensor_scalar(q2_unit[:], hinv[:, 3:4], -B_SCALE, None, ALU.mult)
                ins.then_inc(scales_ready, 1)


            def layernorm1(g):
                dve.wait_ge(x_loaded, count(g, 16, 16))
                for b in range(GB):
                    ins = nc.vector.bn_stats(bn1[:, b, :], xin[:, b, :])
                ins.then_inc(stats1, 1)
                dve.wait_ge(stats1, count(g, 1, 1))
                apart(dve)
                for b in range(GB):
                    ins = nc.vector.bn_aggr(mv1[:, b, :], bn1[:, b, :])
                ins.then_inc(moments1, 1)

            layernorm1(0)
            weight_scales(0)
            for n in range(A_RAW):
                split_lo(n)
            weight_scales(1)
            dve.wait_ge(scales_ready, 2)
            dve.wait_ge(consts_loaded, 16 * (len(rows) + 4))
            nc.vector.tensor_scalar(bq_neg[:], bqk_col[:, 0:KC], -B_SCALE, None, ALU.mult).then_inc(bias_scaled, 1)
            nc.vector.tensor_scalar(conv_neg[:], conv_in[:], -B_SCALE, None, ALU.mult).then_inc(bias_scaled, 1)
            dve.wait_ge(bias_scaled, 2)
            nc.vector.scalar_tensor_tensor(out=conv_b0[:], in0=bqk_col[:, 0:1], scalar=conv_neg[:, 1:2],
                                           in1=conv_neg[:, 3:4], op0=ALU.mult, op1=ALU.add).then_inc(bias_scaled, 1)
            nc.vector.tensor_tensor(conv_mid[:], conv_neg[:, 1:2], hinv[:, 3:4], ALU.mult).then_inc(bias_scaled, 1)

            def gate(part, g):
                k = [(0, 6, 12)[part]]

                def link(ins):
                    ins.then_inc(gate_step, 1)
                    k[0] += 1
                    dve.wait_ge(gate_step, count(g, GATE_LINKS, k[0]))

                def over_e(t):
                    return t[:].rearrange("p e b -> p b e")

                def each_e(col):
                    return col[:].unsqueeze(1).broadcast_to([P, NE, GB])

                logit, shifted, e1, gates, d2, e2, above, lowest, sel = g_tmp
                lmax, esum, einv, gmax, gmin, wsum, winv = g_col
                v = nc.vector
                if part == 0:
                    wait_evacuated(dve, ("B", "v", GB - 1, 0), g)
                    link(v.tensor_scalar(g_hid[:], V2[:, :, C:VG], 0.0, None, ALU.max))
                    for e in range(NE):
                        ins = v.tensor_tensor(g_prod[:, e], g_hid[:],
                                              wg2_row[:, e, :].unsqueeze(1).broadcast_to([P, GB, GH]), ALU.mult)
                    link(ins)
                    link(v.tensor_reduce(sel[:], g_prod, AXX, ALU.add))
                    link(v.tensor_tensor(logit[:], sel[:], bg2_row[:].unsqueeze(2).broadcast_to([P, NE, GB]), ALU.add))
                    ins = v.tensor_reduce(lmax[:], over_e(logit), AXX, ALU.max)
                    link(ins)
                    v.tensor_tensor(shifted[:], logit[:], each_e(lmax), ALU.subtract).then_inc(gate_step, 1)
                elif part == 1:
                    dve.wait_ge(gate_exp, count(g, 2, 1))
                    link(v.tensor_reduce(esum[:], over_e(e1), AXX, ALU.add))
                    link(v.reciprocal(einv[:], esum[:]))
                    link(v.tensor_tensor(gates[:], e1[:], each_e(einv), ALU.mult))
                    v.tensor_reduce(gmin[:], over_e(gates), AXX, ALU.min)
                    link(v.tensor_reduce(gmax[:], over_e(gates), AXX, ALU.max))
                    v.tensor_tensor(d2[:], gates[:], each_e(gmax), ALU.subtract).then_inc(gate_step, 1)
                    v.tensor_tensor(above[:], gates[:], each_e(gmin), ALU.not_equal)
                    v.tensor_tensor(lowest[:], gates[:], each_e(gmin), ALU.is_equal).then_inc(gate_step, 1)
                else:
                    dve.wait_ge(gate_step, count(g, GATE_LINKS, 12))
                    v.tensor_copy(sel[:, 2, :], above[:, 2, :])
                    link(v.tensor_tensor(sel[:, 0:2, :], above[:, 0:2, :], lowest[:, 1:3, :], ALU.max))
                    link(v.tensor_tensor(sel[:, 0, :], sel[:, 0, :], lowest[:, 2, :], ALU.max))
                    dve.wait_ge(gate_exp, count(g, 2, 2))
                    link(v.tensor_tensor(gates[:], e2[:], sel[:], ALU.mult))
                    link(v.tensor_reduce(wsum[:], over_e(gates), AXX, ALU.add))
                    link(v.reciprocal(winv[:], wsum[:]))
                    link(v.tensor_tensor(g_w[:], gates[:], each_e(winv), ALU.mult))

            def do(step, g, last):
                stage, kind, b, c = step
                A = stage == "A"
                src = bank_of(step) if kind in EVAC else None
                freed = evacuated[counted(step), "dve"]
                if kind == "hT":
                    wait_hi(dve, step, g)
                    nc.vector.scalar_tensor_tensor(out=hT_lo[:, b, :], in0=src[:, :], scalar=H_SCALE,
                                                   in1=hT_hi[:, b, :], op0=ALU.mult, op1=ALU.subtract)\
                        .then_inc(freed, 1)
                elif kind == "qk":
                    wait_hi(dve, step, g)
                    hi, lo = ((q_parts, k_parts)[b // KC][n][:, b % KC, :] for n in range(2))
                    nc.vector.scalar_tensor_tensor(out=lo, in0=src[:, :], scalar=-QK_SHIFT if b < KC else QK_SHIFT,
                                                   in1=hi, op0=ALU.mult, op1=ALU.subtract).then_inc(freed, 1)
                    if static_zero(g) and b == 2 * KC - 1:
                        for n in range(A_RAW, 8):
                            split_lo(n)
                        dve.wait_ge(w_lo, 8)
                        dve.wait_ge(consts_built, 1)
                elif kind == "mix":
                    wait_hi(dve, step, g)
                    hi, lo = (oT_hi[b % 2], oT_lo[b % 2]) if A else (yT_hi[b % 2], yT_lo[b % 2])
                    nc.vector.tensor_tensor(lo[:].rearrange("p c t -> p (c t)"), src[:, 0:C],
                                            hi[:].rearrange("p c t -> p (c t)").bitcast(F32),
                                            ALU.subtract).then_inc(freed, 1)
                elif kind == "v":
                    wait_products(dve, step, g)
                    V_b, row, col = (V[:, b, :], bv_row, 2) if A else (V2[:, b, :], bvg_row, 5)
                    nc.vector.scalar_tensor_tensor(out=V_b, in0=src[:, 0:row.shape[1]], scalar=hinv[:, col:col + 1],
                                                   in1=row[:], op0=ALU.mult, op1=ALU.add).then_inc(freed, 1)
                elif kind == "score" and A:
                    if b == 0 and c == 0:
                        dve.wait_ge(adj_scaled, count(g, 1, 1))
                    wait_products(dve, step, g)
                    apart(dve)
                    for j in range(HPC):
                        h = c * HPC + j
                        ins = nc.vector.tensor_tensor_reduce(
                            S[b % 2][:, h, :], src[:, j * T:(j + 1) * T], adj2[:, b, :], 1.0, 3.0e38,
                            ALU.add, ALU.min, smin[b % 2][:, h:h + 1])
                    ins.then_inc(biased, 1)
                    dve.wait_ge(biased, count(g, GB * KC, b * KC + c + 1))
                    hs = slice(c * HPC, (c + 1) * HPC)
                    nc.vector.tensor_scalar(sbias[b % 2][:, hs], smin[b % 2][:, hs], s_unit[:], None, ALU.mult)
                    nc.vector.tensor_reduce(smax[b % 2][:, hs], S[b % 2][:, hs, :], AXX, ALU.max).then_inc(freed, 1)
                elif kind == "score":
                    wait_products(dve, step, g)
                    apart(dve)
                    for e in range(NE):
                        ins = nc.vector.tensor_tensor_reduce(
                            S2[b % 2][:, e, :], src[:, e * T:(e + 1) * T], later[:], 1.0, 3.0e38,
                            ALU.add, ALU.min, s2min[b % 2][:, e:e + 1])
                    ins.then_inc(freed, 1)
                elif kind == "norm" and A:
                    k = b % 2
                    nc.vector.tensor_scalar(live[k][:], smin[k][:], 0.0, None, ALU.not_equal).then_inc(guard, 1)
                    dve.wait_ge(guard, count(g, 2 * GB, 2 * b + 1))
                    dve.wait_ge(exped, count(g, GB, b + 1))
                    nc.vector.reciprocal(rinv[k][:], ssum[k][:])
                    nc.vector.scalar_tensor_tensor(out=live2[k][:], in0=smax[k][:], scalar=0.0, in1=live[k][:],
                                                   op0=ALU.not_equal, op1=ALU.max).then_inc(guard, 1)
                    dve.wait_ge(guard, count(g, 2 * GB, 2 * b + 2))
                    nc.vector.tensor_tensor(rowf[k][:], rinv[k][:], live2[k][:], ALU.mult).then_inc(row_factor, 1)
                elif kind == "norm":
                    k = b % 2
                    dve.wait_ge(exped2, count(g, GB, b + 1))
                    nc.vector.reciprocal(r2inv[k][:], s2sum[k][:]).then_inc(sums_inverted2, 1)
                    dve.wait_ge(sums_inverted2, count(g, GB, b + 1))
                    dve.wait_ge(gate_step, count(g, GATE_LINKS, GATE_LINKS))
                    nc.vector.tensor_tensor(row2f[k][:], r2inv[k][:], g_w[:, :, b], ALU.mult).then_inc(row_factor2, 1)
                elif kind == "proj" and A:
                    wait_products(dve, step, g)
                    dve.wait_ge(xres_ready, count(g, 1, 1))
                    if not static_zero(g):
                        dve.wait_ge(x1res_ready, count(g, 1, 0))
                    nc.vector.tensor_tensor(x1[:, b, :], src[:, 0:C], xres[:, b, :], ALU.add).then_inc(freed, 1)
                elif kind == "proj":
                    wait_products(dve, step, g)
                    dve.wait_ge(x1res_ready, count(g, 1, 1))
                    nc.vector.tensor_tensor(x1res[:, b, :], src[:, 0:C], x1res[:, b, :], ALU.add).then_inc(freed, 1)
                elif kind == "ln2":
                    wait_evacuated(dve, ("A", "proj", b, 0), g)
                    nc.vector.bn_stats(bn2[:, b, :], x1[:, b, :]).then_inc(stats2, 1)
                    dve.wait_ge(stats2, count(g, GB, b + 1))
                    apart(dve)
                    nc.vector.bn_aggr(mv2[:, b, :], bn2[:, b, :]).then_inc(moments2, 1)
                elif kind == "ln1" and not last:
                    layernorm1(following(g))
                elif kind == "conv":
                    wait_evacuated(dve, ("B", "qk", 0, 0), g)
                    q = q2[:, 0, :].rearrange("p (b t) -> p b t", b=GB)
                    r = q2raw[:].rearrange("p (b t) -> p b t", b=GB)
                    nc.vector.scalar_tensor_tensor(out=q[:, :, 1:T], in0=r[:, :, 0:T - 1], scalar=conv_neg[:, 0:1],
                                                   in1=q[:, :, 1:T], op0=ALU.mult, op1=ALU.add).then_inc(conv_step, 1)
                    dve.wait_ge(conv_step, count(g, 2, 1))
                    nc.vector.scalar_tensor_tensor(out=q[:, :, 0:T - 1], in0=r[:, :, 1:T], scalar=conv_neg[:, 2:3],
                                                   in1=q[:, :, 0:T - 1], op0=ALU.mult, op1=ALU.add).then_inc(conv_step, 1)
                elif kind == "gate":
                    gate(b, g)

            groups(dve, "dve", do)

        @block.gpsimd
        def _(pool):
            nc.gpsimd.memset(ident[:], 0.0)
            nc.gpsimd.memset(half[:], -0.5)
            nc.gpsimd.memset(later[:], 0.0).then_inc(consts_zeroed, 1)
            pool.wait_ge(consts_zeroed, 1)
            nc.gpsimd.affine_select(out=later[:], in_=later[:], compare_op=ALU.is_ge, fill=MASKED, base=0,
                                    pattern=[[-1, P]], channel_multiplier=1)
            nc.gpsimd.affine_select(out=ident[:], in_=ident[:], compare_op=ALU.not_equal, fill=1.0, base=0,
                                    pattern=[[-1, P]], channel_multiplier=1).then_inc(consts_built, 1)
            pool.wait_ge(consts_built, 1)

            def scale_adj(g):
                pool.wait_ge(adj_loaded, count(g, 16, 16))
                apart(pool)
                nc.gpsimd.tensor_scalar(adj2[:], adj2[:], adj_unit[:], None, ALU.mult).then_inc(adj_scaled, 1)

            def layernorm1(g):
                pool.wait_ge(moments1, count(g, 1, 1))
                apart(pool)
                nc.gpsimd.tensor_scalar(ve1[:], mv1[:, :, 1], EPS, None, ALU.add).then_inc(vareps1, 1)
                pool.wait_ge(vareps1, count(g, 1, 1))
                nc.gpsimd.tensor_tensor(rstd1[:], ve1[:], half[:], ALU.pow).then_inc(rstd1_done, 1)
                pool.wait_ge(rstd1_done, count(g, 1, 1))
                apart(pool)
                for b in range(GB):
                    ins = nc.gpsimd.tensor_scalar(h1[:, b, :], xin[:, b, :], mv1[:, b, 0:1], rstd1[:, b:b + 1],
                                                  ALU.subtract, ALU.mult)
                ins.then_inc(h1_ready, 1)

            layernorm1(0)
            for n in range(2):
                pool.wait_ge(maxima, n + 1)
                nc.gpsimd.partition_all_reduce(wtop[:, 3 * n:3 * n + 3], wmax[:, 3 * n:3 * n + 3], P,
                                               bass.bass_isa.ReduceOp.max).then_inc(tops, 1)
            pool.wait_ge(scales_ready, 1)
            scale_adj(0)
            pool.wait_ge(consts_loaded, 16 * (len(rows) + 4))
            pool.wait_ge(w_lo, 8)

            def do(step, g, last):
                stage, kind, b, c = step
                A = stage == "A"
                if kind == "res" and A:
                    if not static_zero(g):
                        wait_evacuated(pool, ("A", "proj", GB - 1, 0), before(g))
                    nc.gpsimd.tensor_tensor(xres[:], xin[:], bo_row[:].unsqueeze(1).broadcast_to([P, GB, C]),
                                            ALU.add).then_inc(xres_ready, 1)
                elif kind == "res":
                    wait_evacuated(pool, ("A", "proj", GB - 1, 0), g)
                    pool.wait_ge(moments2, count(g, GB, GB))
                    if not static_zero(g):
                        pool.wait_ge(stored, count(g, 16 * GB, 0))
                    nc.gpsimd.tensor_tensor(x1res[:], x1[:], bp_row[:].unsqueeze(1).broadcast_to([P, GB, C]),
                                            ALU.add).then_inc(x1res_ready, 1)
                elif kind == "norm" and A:
                    pool.wait_ge(row_factor, count(g, GB, b + 1))
                    for n in range(KC):
                        hs = slice(n * HPC, (n + 1) * HPC)
                        nc.gpsimd.tensor_tensor(S[b % 2][:, hs, :], S[b % 2][:, hs, :],
                                                rowf[b % 2][:, hs].unsqueeze(2).broadcast_to([P, HPC, T]),
                                                ALU.mult).then_inc(normed, 1)
                elif kind == "norm":
                    pool.wait_ge(row_factor2, count(g, GB, b + 1))
                    nc.gpsimd.tensor_tensor(S2[b % 2][:], S2[b % 2][:],
                                            row2f[b % 2][:].unsqueeze(2).broadcast_to([P, NE, T]),
                                            ALU.mult).then_inc(normed2, 1)
                elif kind == "ln2":
                    pool.wait_ge(moments2, count(g, GB, b + 1))
                    apart(pool)
                    nc.gpsimd.tensor_scalar(ve2[:, b:b + 1], mv2[:, b, 1:2], EPS, None, ALU.add).then_inc(vareps2, 1)
                    pool.wait_ge(vareps2, count(g, GB, b + 1))
                    nc.gpsimd.tensor_tensor(rstd2[:, b:b + 1], ve2[:, b:b + 1], half[:, 0:1],
                                            ALU.pow).then_inc(rstd2_done, 1)
                    pool.wait_ge(rstd2_done, count(g, GB, b + 1))
                    apart(pool)
                    nc.gpsimd.tensor_scalar(h2[:, b, :], x1[:, b, :], mv2[:, b, 0:1], rstd2[:, b:b + 1],
                                            ALU.subtract, ALU.mult).then_inc(h2_ready, 1)
                elif kind == "ln1" and not last:
                    wait_products(pool, ("A", "hT", KC - 1, 0), g)
                    layernorm1(following(g))
                elif kind == "adj" and not last:
                    scale_adj(following(g))

            groups(pool, "pool", do)


def kernel(**inputs):
    import numpy as np
    import concourse.bacc as bacc
    from concourse.bass_utils import run_bass_kernel_spmd

    def rows(w):
        w = np.asarray(w)
        return np.ascontiguousarray(w.reshape(w.shape[0] // P, P, w.shape[1]).transpose(1, 0, 2))

    def flat(name):
        return np.ascontiguousarray(np.asarray(inputs[name]).reshape(-1))

    a, f = "L0_gnn_", "L0_ffn_"
    wv2 = np.asarray(inputs[f + "Wv"]).transpose(1, 0, 2).reshape(C, C)
    arrays = {
        "x": np.ascontiguousarray(inputs["x"]),
        "adj": np.ascontiguousarray(inputs["adj"]),
        "wq": rows(np.asarray(inputs[a + "Wq"]).T),
        "wk": rows(np.asarray(inputs[a + "Wk"]).T),
        "wv": rows(np.asarray(inputs[a + "Wv"]).T),
        "wo": rows(np.asarray(inputs[a + "Wo"]).T),
        "a_bv": flat(a + "bv"),
        "a_bo": flat(a + "bo"),
        "wqk": rows(inputs[f + "Wqk"]),
        "bqk": np.ascontiguousarray(np.asarray(inputs[f + "bqk"]).reshape(2 * KC, P).T),
        "wv2": rows(wv2),
        "wg1": rows(inputs[f + "Wg1"]),
        "wp": rows(inputs[f + "Wp"]),
        "b_bv": flat(f + "bv"),
        "bg1": flat(f + "bg1"),
        "wg2": np.ascontiguousarray(np.asarray(inputs[f + "Wg2"]).T),
        "bg2": flat(f + "bg2"),
        "b_bp": flat(f + "bp"),
        "conv_w": np.ascontiguousarray(np.asarray(inputs[f + "conv_w"]).reshape(P, 3)),
        "conv_b": np.ascontiguousarray(np.asarray(inputs[f + "conv_b"]).reshape(P, 1)),
    }
    nc = bacc.Bacc("TRN2", target_bir_lowering=False, num_devices=1)
    aps = {n: nc.dram_tensor(f"in_{n}", v.shape, F32, kind="ExternalInput").ap() for n, v in arrays.items()}
    out = nc.dram_tensor("out", (NB, T, C), F32, kind="ExternalOutput").ap()
    build(nc, out=out, **aps)
    r = run_bass_kernel_spmd(nc, [{f"in_{n}": v for n, v in arrays.items()}], core_ids=[0])
    return r.results[0]["out"]
```
